# Optimizing a Trainium2 kernel written in Bass

```python
import numpy as np
import jax
import jax.numpy as jnp

def _softmax(x, axis=-1):
    return jax.nn.softmax(x, axis=axis)

def _gelu(x):
    return jax.nn.gelu(x, approximate=True)

def _silu(x):
    return jax.nn.silu(x)

def _sigmoid(x):
    return jax.nn.sigmoid(x)

def _layernorm(x, axis=-1, eps=1e-05):
    m = jnp.mean(x, axis=axis, keepdims=True)
    v = jnp.var(x, axis=axis, keepdims=True)
    return (x - m) / jnp.sqrt(v + eps)

def _scatter_add(tgt, idx, src, axis=0):
    return tgt.at[idx].add(src)

def _segment_sum(src, seg, n):
    return jax.ops.segment_sum(src, seg, n)
kernel_name = 'mk_seq_preln_d1_jaxref_r8_3541b8'

def setup_inputs(seed: int=0):
    np.random.seed(seed)
    _w = jnp.asarray

    def _L0_attn_setup():
        import jax, jax.numpy as jnp
        import numpy as np
        B, S, DIM = (4, 512, 128)
        ERR_CLIP = 5.0
        GRAD_CLIP = 1.0
        INIT_STD = 0.02

        def _silu_deriv(x):
            s = jax.nn.sigmoid(x)
            return s * (1.0 + x * (1.0 - s))

        def _forward(x, Wk, Wv, Wq, Wout, W0, W1, Wg_decay, bg_decay, Wg_lr, bg_lr, Wg_mom, bg_mom):
            k = x @ Wk.T
            v = x @ Wv.T
            q = x @ Wq.T
            alpha = jax.nn.sigmoid(jnp.mean(x @ Wg_decay.T + bg_decay))
            lr = jax.nn.sigmoid(jnp.mean(x @ Wg_lr.T + bg_lr))
            eta = jax.nn.sigmoid(jnp.mean(x @ Wg_mom.T + bg_mom))
            W0d = jax.lax.stop_gradient(W0)
            W1d = jax.lax.stop_gradient(W1)
            pre1 = k @ W0d.T
            a1 = jax.nn.silu(pre1)
            pred = a1 @ W1d.T
            scale = 2.0 / float(S)
            err = jnp.clip(pred - v, -ERR_CLIP, ERR_CLIP)
            d2 = scale * err
            g1 = jnp.clip(jnp.einsum('bsd,bse->de', d2, a1), -GRAD_CLIP, GRAD_CLIP)
            d1 = d2 @ W1d * _silu_deriv(pre1)
            g0 = jnp.clip(jnp.einsum('bsd,bse->de', d1, k), -GRAD_CLIP, GRAD_CLIP)
            m0 = eta * jnp.zeros_like(W0) - lr * g0
            m1 = eta * jnp.zeros_like(W1) - lr * g1
            W0n = (1.0 - alpha) * W0 + m0
            W1n = (1.0 - alpha) * W1 + m1
            h = jax.nn.silu(q @ W0n.T) @ W1n.T
            return h @ Wout.T
        key = jax.random.key(seed)
        ks = jax.random.split(key, 10)
        fan = 1.0 / np.sqrt(DIM)
        return {'x': jax.random.normal(ks[0], (B, S, DIM), jnp.float32), 'Wk': jax.random.normal(ks[1], (DIM, DIM), jnp.float32) * INIT_STD, 'Wv': jax.random.normal(ks[2], (DIM, DIM), jnp.float32) * INIT_STD, 'Wq': jax.random.normal(ks[3], (DIM, DIM), jnp.float32) * INIT_STD, 'Wout': jax.random.normal(ks[4], (DIM, DIM), jnp.float32) * INIT_STD, 'W0': jax.random.normal(ks[5], (DIM, DIM), jnp.float32) * fan, 'W1': jax.random.normal(ks[6], (DIM, DIM), jnp.float32) * fan, 'Wg_decay': jax.random.normal(ks[7], (1, DIM), jnp.float32) * INIT_STD, 'bg_decay': jnp.full((1,), -4.0, jnp.float32), 'Wg_lr': jax.random.normal(ks[8], (1, DIM), jnp.float32) * INIT_STD, 'bg_lr': jnp.zeros((1,), jnp.float32), 'Wg_mom': jax.random.normal(ks[9], (1, DIM), jnp.float32) * INIT_STD, 'bg_mom': jnp.zeros((1,), jnp.float32)}
    _L0_attn_in = _L0_attn_setup()

    def _L0_ffn_setup():
        import jax, jax.numpy as jnp
        import numpy as np
        N_EXPERTS = 8
        CAP_FACTOR = 1.25
        BATCH, SEQ, DMODEL, DFF = (4, 256, 128, 512)
        key = jax.random.key(seed)
        k0, k1, k2, k3 = jax.random.split(key, 4)
        x = jax.random.normal(k0, (BATCH, SEQ, DMODEL), dtype=jnp.float32)
        Wr = jax.random.normal(k1, (DMODEL, N_EXPERTS), dtype=jnp.float32) * 0.02
        W1 = jax.random.normal(k2, (N_EXPERTS, DMODEL, DFF), dtype=jnp.float32) * 0.02
        W2 = jax.random.normal(k3, (N_EXPERTS, DFF, DMODEL), dtype=jnp.float32) * 0.02
        return {'x': x, 'Wr': Wr, 'W1': W1, 'W2': W2}
    _L0_ffn_in = _L0_ffn_setup()
    _d = {'L0_attn_x': _L0_attn_in['x'], 'L0_attn_Wk': _L0_attn_in['Wk'], 'L0_attn_Wv': _L0_attn_in['Wv'], 'L0_attn_Wq': _L0_attn_in['Wq'], 'L0_attn_Wout': _L0_attn_in['Wout'], 'L0_attn_W0': _L0_attn_in['W0'], 'L0_attn_W1': _L0_attn_in['W1'], 'L0_attn_Wg_decay': _L0_attn_in['Wg_decay'], 'L0_attn_bg_decay': _L0_attn_in['bg_decay'], 'L0_attn_Wg_lr': _L0_attn_in['Wg_lr'], 'L0_attn_bg_lr': _L0_attn_in['bg_lr'], 'L0_attn_Wg_mom': _L0_attn_in['Wg_mom'], 'L0_attn_bg_mom': _L0_attn_in['bg_mom'], 'L0_ffn_Wr': _L0_ffn_in['Wr'], 'L0_ffn_W1': _L0_ffn_in['W1'], 'L0_ffn_W2': _L0_ffn_in['W2']}
    _x0 = _d['L0_attn_x']
    _d['L0_attn_x'] = jax.random.normal(jax.random.fold_in(jax.random.key(seed), 1), (16, 256, 128), dtype=_x0.dtype)
    del _x0
    return _d

def reference(L0_attn_x, L0_attn_Wk, L0_attn_Wv, L0_attn_Wq, L0_attn_Wout, L0_attn_W0, L0_attn_W1, L0_attn_Wg_decay, L0_attn_bg_decay, L0_attn_Wg_lr, L0_attn_bg_lr, L0_attn_Wg_mom, L0_attn_bg_mom, L0_ffn_Wr, L0_ffn_W1, L0_ffn_W2):

    def _L0_attn_ref(x, Wk, Wv, Wq, Wout, W0, W1, Wg_decay, bg_decay, Wg_lr, bg_lr, Wg_mom, bg_mom):
        import jax, jax.numpy as jnp
        import numpy as np
        B, S, DIM = (4, 512, 128)
        ERR_CLIP = 5.0
        GRAD_CLIP = 1.0
        INIT_STD = 0.02

        def _silu_deriv(x):
            s = jax.nn.sigmoid(x)
            return s * (1.0 + x * (1.0 - s))

        def _forward(x, Wk, Wv, Wq, Wout, W0, W1, Wg_decay, bg_decay, Wg_lr, bg_lr, Wg_mom, bg_mom):
            k = x @ Wk.T
            v = x @ Wv.T
            q = x @ Wq.T
            alpha = jax.nn.sigmoid(jnp.mean(x @ Wg_decay.T + bg_decay))
            lr = jax.nn.sigmoid(jnp.mean(x @ Wg_lr.T + bg_lr))
            eta = jax.nn.sigmoid(jnp.mean(x @ Wg_mom.T + bg_mom))
            W0d = jax.lax.stop_gradient(W0)
            W1d = jax.lax.stop_gradient(W1)
            pre1 = k @ W0d.T
            a1 = jax.nn.silu(pre1)
            pred = a1 @ W1d.T
            scale = 2.0 / float(S)
            err = jnp.clip(pred - v, -ERR_CLIP, ERR_CLIP)
            d2 = scale * err
            g1 = jnp.clip(jnp.einsum('bsd,bse->de', d2, a1), -GRAD_CLIP, GRAD_CLIP)
            d1 = d2 @ W1d * _silu_deriv(pre1)
            g0 = jnp.clip(jnp.einsum('bsd,bse->de', d1, k), -GRAD_CLIP, GRAD_CLIP)
            m0 = eta * jnp.zeros_like(W0) - lr * g0
            m1 = eta * jnp.zeros_like(W1) - lr * g1
            W0n = (1.0 - alpha) * W0 + m0
            W1n = (1.0 - alpha) * W1 + m1
            h = jax.nn.silu(q @ W0n.T) @ W1n.T
            return h @ Wout.T
        return _forward(x, Wk, Wv, Wq, Wout, W0, W1, Wg_decay, bg_decay, Wg_lr, bg_lr, Wg_mom, bg_mom)

    def _L0_ffn_ref(x, Wr, W1, W2):
        import jax, jax.numpy as jnp
        import numpy as np
        N_EXPERTS = 8
        CAP_FACTOR = 1.25
        BATCH, SEQ, DMODEL, DFF = (4, 256, 128, 512)
        B, S, D = x.shape
        E = W1.shape[0]
        cap = int(CAP_FACTOR * B * S / E)
        t = x.reshape(-1, D)
        probs = jax.nn.softmax(t @ Wr, axis=-1)
        idx = jnp.argmax(probs, axis=-1)
        pmax = jnp.max(probs, axis=-1)
        onehot = jax.nn.one_hot(idx, E, dtype=jnp.int32)
        pos = jnp.sum(jnp.cumsum(onehot, axis=0) * onehot, axis=-1) - 1
        kept = pos < cap
        flat = idx * cap + jnp.minimum(pos, cap - 1)
        disp = jnp.zeros((E * cap, D), t.dtype).at[flat].add(t * kept[:, None].astype(t.dtype))
        ein = disp.reshape(E, cap, D)
        h = jax.nn.relu(jnp.einsum('ecd,edf->ecf', ein, W1))
        eout = jnp.einsum('ecf,efd->ecd', h, W2).reshape(E * cap, D)
        comb = jnp.where(kept[:, None], eout[flat], t)
        factor = jnp.where(kept, pmax, jnp.ones_like(pmax))
        out = (comb * factor[:, None]).reshape(B, S, D)
        return out
    x = L0_attn_x
    x = x + _L0_attn_ref(_layernorm(x, axis=-1), L0_attn_Wk, L0_attn_Wv, L0_attn_Wq, L0_attn_Wout, L0_attn_W0, L0_attn_W1, L0_attn_Wg_decay, L0_attn_bg_decay, L0_attn_Wg_lr, L0_attn_bg_lr, L0_attn_Wg_mom, L0_attn_bg_mom)
    x = x + _L0_ffn_ref(_layernorm(x, axis=-1), L0_ffn_Wr, L0_ffn_W1, L0_ffn_W2)
    return x

_drawn_inputs = setup_inputs


def setup_inputs(seed=0):
    import zlib

    import numpy as np

    out = dict(_drawn_inputs(seed))
    spreads = {}
    factors = {'L0_attn_Wk': 4.155,
     'L0_attn_Wv': 4.824,
     'L0_attn_W0': 3.104,
     'L0_attn_W1': 3.146,
     'L0_attn_Wg_decay': 64.0,
     'L0_attn_Wg_lr': 28.81,
     'L0_ffn_Wr': 4.766,
     'L0_ffn_W1': 5.471,
     'L0_ffn_W2': 4.553}
    for name, (base, spread) in spreads.items():
        noise = np.random.default_rng([zlib.crc32(name.encode()), seed]).standard_normal(out[name].shape)
        drawn = base * np.exp(spread * noise) if base else spread * noise
        out[name] = jnp.asarray(drawn.astype(out[name].dtype))
    for name, factor in factors.items():
        out[name] = (out[name] * factor).astype(out[name].dtype)
    return out
```

```python
from contextlib import ExitStack

import numpy as np

import concourse.bass as bass
from concourse import mybir

ALU = mybir.AluOpType
ACT = mybir.ActivationFunctionType
F32 = mybir.dt.float32
BF16 = mybir.dt.bfloat16
I32 = mybir.dt.int32
U32 = mybir.dt.uint32
AX = mybir.AxisListType.X

P = 128
EPS = 1e-5
ERR_CLIP = 5.0
GRAD_CLIP = 1.0
SCALE = 2.0 / 512.0
CAP_FACTOR = 1.25
GROUP = 4
WK, WKT, WVT, WQ, W0T, W1N, W1T, WOT = range(8)


def build(nc: bass.Bass, x: bass.AP, wpack: bass.AP, wsmall: bass.AP, biases: bass.AP,
          w_up: bass.AP, w_down: bass.AP, out: bass.AP):
    T, D = x.shape
    E, _, F = w_up.shape
    assert D == P
    TILES = T // P
    NB = TILES // GROUP
    COLS = GROUP * P
    CAP = int(CAP_FACTOR * T / E)
    ST = CAP // P
    HALF = CAP // 2
    FC = F // P
    assert NB == 8 and E == 8 and CAP == ST * P and HALF <= 512 and FC == 4
    C_MEAN, C_VAR, C_D, C_ID = D, D + 1, D + 2, D + 2 + E
    ROW = C_ID + 1
    NO_SLOT = float(2 ** 20)
    NO_TOKEN = float(T)

    disp = nc.dram_tensor("disp", [E * CAP, ROW], F32, kind="Internal").ap()

    with ExitStack() as ctx:
        def sb(name, shape, dt=F32):
            return ctx.enter_context(nc.sbuf_tensor(name, shape, dt))

        def sem(name):
            return ctx.enter_context(nc.semaphore(name))

        bank = [ctx.enter_context(nc.psum_tensor(f"bank{i}", [P, 512], F32)) for i in range(8)]

        ident = sb("ident", [P, P])
        centre = sb("centre", [P, P])
        upper = sb("upper", [P, P], BF16)
        ones = sb("ones", [P, P], BF16)
        zeros = sb("zeros", [P, 2 * P])
        neg_half = sb("neg_half", [P, TILES // 2])
        eps = sb("eps", [P, TILES // 2])
        rank = sb("rank", [P, E])
        wts = sb("wts", [P, 8 * P])
        gw = sb("gw", [P, 3 + E])
        gate_w = sb("gate_w", [P, 3 * P])
        gate_b = sb("gate_b", [P, 3])
        a_w = sb("a_w", [P, P])
        nwv = sb("nwv", [P, P])
        wr_c = sb("wr_c", [P, E])
        xr = sb("xr", [P, TILES * P])
        stat = sb("stat", [P, GROUP, 6])
        mv = sb("mv", [P, 2, GROUP, 2])
        veps = sb("veps", [P, TILES // 2])
        rs = sb("rs", [P, 2, GROUP])
        xn = sb("xn", [P, 2, COLS])
        xnt = sb("xnt", [P, COLS])
        xnt_all = sb("xnt_all", [P, T])
        xsum = sb("xsum", [P, NB])
        sg = sb("sg", [P, 2, COLS])
        a1 = sb("a1", [P, 2, COLS])
        ds1 = sb("ds1", [P, COLS])
        ds = sb("ds", [P, 2, COLS])
        a1t = sb("a1t", [P, COLS])
        er = sb("er", [P, COLS])
        ert = sb("ert", [P, COLS])
        d1 = sb("d1", [P, COLS])
        gl = sb("gl", [P, 3])
        gp = sb("gp", [P, 3])
        gs = sb("gs", [P, 3])
        gk = sb("gk", [P, 3])
        base0 = sb("base0", [P, P])
        base1 = sb("base1", [P, P])
        gt = sb("gt", [P, P])
        c0 = sb("c0", [P, P])
        c1 = sb("c1", [P, P])
        w0n = sb("w0n", [P, P])
        w1n = sb("w1n", [P, P])
        mz = sb("mz", [P, P])
        n2 = sb("n2", [P, P])
        st = sb("st", [P, COLS])
        rows = sb("rows", [P, TILES, ROW])
        stat2 = sb("stat2", [P, GROUP, 6])
        mv2 = sb("mv2", [P, GROUP, 2])
        x1t = sb("x1t", [P, COLS])
        mx = sb("mx", [P, GROUP])
        cand = sb("cand", [P, GROUP, E])
        best = sb("best", [P, GROUP])
        hot = sb("hot", [P, 2, GROUP + 1, E], BF16)
        own = sb("own", [P, GROUP, E])
        pos = sb("pos", [P, GROUP])
        slot = sb("slot", [P, GROUP])
        over = sb("over", [P, GROUP])
        idx = sb("idx", [P, TILES], I32)
        rs2 = sb("rs2", [P, TILES])
        rs2p = sb("rs2p", [P, TILES])
        nmr2 = sb("nmr2", [P, TILES])
        empty = sb("empty", [P, ST, ROW])
        dr = sb("dr", [P, E, ST, ROW])
        ids = sb("ids", [P, 2, ST], I32)
        ve3 = sb("ve3", [P, ST])
        rs3 = sb("rs3", [P, 2, ST])
        tn = sb("tn", [P, CAP])
        tt = sb("tt", [P, CAP])
        dd = sb("dd", [P, ST, E])
        th = sb("th", [P, ST, E])
        den = sb("den", [P, ST, E])
        rat = sb("rat", [P, ST, E])
        esum = sb("esum", [P, ST])
        pm = sb("pm", [P, ST])
        w1r = sb("w1r", [P, 2, F])
        w2r = sb("w2r", [P, 2, FC, P])
        ht = sb("ht", [P, FC, CAP])
        orow = sb("orow", [P, 2, ST, P])
        warm = sb("warm", [P, 2])
        spare = sb("spare", [P, 5])

        def w(k):
            return wts[:, k * P:(k + 1) * P]

        def tile(t, g):
            return t[:, g * P:(g + 1) * P]

        names = """wts_loaded small_loaded ident_ready consts_ready zeros_ready dve_consts empty_ready disp_init
            mv_stat mv_ready veps_ready rstd_ready xn_ready xt_done xnt_ready copied pre_done sig_ready a1_ready
            at_done a1t_ready err_done clip_ready et_done ert_ready dw_done ds1_ready ds_ready d1_ready g1_done
            gt_done setup_mm setup_ready gates_mm gate_step gates_ready upd_step gt_ready g0_mm w0_ready w1_ready
            mz_mm mz_ready n2_ready z_done silu_ready o_done x1_ready x1t_done x1t_ready lg_done
            mx_ready d_ready cand_ready best_ready hot_ready count_ready pos_mm own_ready pos_ready slot_ready
            over_ready idx_ready stat2_done mv2_ready scattered ve2_ready rs2_ready nm_ready base_ready base_ready_v
            rows_ids ve3_ready rs3_ready tn_ready tt_mm tt_ready h_mm h_ready y_mm
            dd_ready th_ready den_ready rat_ready esum_ready pm_ready fin_ready warmed""".split()
        S = {n: sem(n) for n in names}
        x_loaded = [sem(f"x_loaded{i}") for i in range(2)]
        base_stored = [sem(f"base_stored{i}") for i in range(2)]
        dr_loaded = [sem(f"dr_loaded{i}") for i in range(2)]
        w1_loaded = [sem(f"w1_loaded{i}") for i in range(2)]
        w2_loaded = [sem(f"w2_loaded{i}") for i in range(2)]
        sent = [sem(f"sent{i}") for i in range(2)]

        def wait(eng, s, count):
            if isinstance(count, int) and count <= 0:
                return
            eng.wait_ge(S[s] if isinstance(s, str) else s, count)


        block = ctx.enter_context(nc.Block())

        @block.sync
        def _(sp):
            def load_x(i, c):
                if isinstance(i, int) and c < 2:
                    pass
                else:
                    sp.wait_ge(x_loaded[c % 2], 16 * (i + c // 2))
                b = 2 * i + c
                sp.dma_start(xr[:, bass.ds(COLS * b, COLS)].rearrange("p (g d) -> p g d", d=P),
                             x_view[:, bass.ds(GROUP * b, GROUP), :]).then_inc(x_loaded[c % 2], 16)

            x_view = x.rearrange("(n p) d -> p n d", p=P)
            out_view = out.rearrange("(n p) d -> p n d", p=P)
            load_x(0, 0)
            sp.dma_start(wts[:], wpack).then_inc(S["wts_loaded"], 16)
            load_x(0, 1)
            sp.dma_start(gw[:], wsmall).then_inc(S["small_loaded"], 16)
            sp.dma_start(gate_b[:], biases.to_broadcast([P, 3])).then_inc(S["small_loaded"], 16)
            with sp.Fori(0, NB // 2 - 1) as i:
                load_x(i, 2)
                load_x(i, 3)
            sp.wait_ge(S["empty_ready"], 2)
            with sp.Fori(0, E) as e:
                sp.dma_start(disp[bass.ds(CAP * e, CAP), :].rearrange("(p s) c -> p s c", s=ST),
                             empty[:]).then_inc(S["disp_init"], 16)

            def load_weights(i, c):
                e = 2 * i + c
                wait(sp, "h_mm", 2 * FC * (e - 1))
                sp.dma_start(w1r[:, c % 2, :], w_up[bass.ds(e, 1)].rearrange("e d f -> d (e f)")
                             ).then_inc(w1_loaded[c % 2], 16)
                wait(sp, "y_mm", e - 1)
                sp.dma_start(w2r[:, c % 2], w_down[bass.ds(e, 1)].rearrange("e (c p) d -> p (e c) d", p=P)
                             ).then_inc(w2_loaded[c % 2], 16)

            def load_rows(i, c):
                if not (isinstance(i, int) and c < 2):
                    sp.wait_ge(dr_loaded[c % 2], 16 * (i + c // 2))
                e = 2 * i + c
                sp.dma_start(dr[:, bass.ds(e, 1)].rearrange("p e s c -> p (e s c)"),
                             disp[bass.ds(CAP * e, CAP), :].rearrange("(p s) c -> p (s c)", s=ST)
                             ).then_inc(dr_loaded[c % 2], 16)

            load_weights(0, 0)
            load_weights(0, 1)

            sp.wait_ge(S["scattered"], 16 * TILES)
            load_rows(0, 0)
            load_rows(0, 1)
            with sp.Fori(0, E // 2 - 1) as i:
                load_rows(i, 2)
                load_rows(i, 3)

            def store_base(k0, n, made, count):
                sp.wait_ge(S[made], count)
                sp.dma_start(out_view[:, k0:k0 + n, :],
                             xr[:, k0 * P:(k0 + n) * P].rearrange("p (g d) -> p g d", d=P)
                             ).then_inc(base_stored[made == "base_ready"], 16)

            BT = TILES // 4
            store_base(0, BT, "base_ready", 1)
            store_base(2 * BT, 2 * BT, "base_ready_v", 1)
            store_base(BT, BT, "base_ready", 2)
            load_weights(0, 2)
            load_weights(0, 3)
            with sp.Fori(1, E // 2 - 1) as i:
                load_weights(i, 2)
                load_weights(i, 3)
            sp.wait_ge(base_stored[0], 16)
            sp.wait_ge(base_stored[1], 32)
            sp.wait_ge(sent[0], 16 * ST * E // 2)
            sp.wait_ge(sent[1], 16 * ST * E // 2)

        @block.gpsimd
        def _(pool):
            g = nc.gpsimd

            def carry(k):
                g.tensor_tensor(spare[:, k:k + 1], eps[:, 0:1], eps[:, 0:1], ALU.add)

            g.memset(ident[:], 0.0).then_inc(S["ident_ready"], 1)
            pool.wait_ge(S["ident_ready"], 1)
            g.affine_select(out=ident[:], in_=ident[:], compare_op=ALU.not_equal, fill=1.0, base=0,
                            pattern=[[-1, P]], channel_multiplier=1).then_inc(S["ident_ready"], 1)
            g.memset(eps[:], EPS)
            g.memset(neg_half[:], -0.5).then_inc(S["consts_ready"], 1)

            def rstd(i, c):
                b = 2 * i + c
                pool.wait_ge(S["mv_ready"], b + 1)
                wait(pool, "rstd_ready", b)
                g.tensor_tensor(veps[:, 0:GROUP], mv[:, c % 2, :, 1], eps[:, 0:GROUP], ALU.add
                                ).then_inc(S["veps_ready"], 1)
                pool.wait_ge(S["veps_ready"], b + 1)
                wait(pool, "xn_ready", b - 1)
                g.tensor_tensor(rs[:, c % 2, :], veps[:, 0:GROUP], neg_half[:, 0:GROUP], ALU.pow
                                ).then_inc(S["rstd_ready"], 1)

            def silu_slope(i, c):
                b = 2 * i + c
                pool.wait_ge(S["a1_ready"], b + 1)
                wait(pool, "ds_ready", b)
                g.tensor_tensor(ds1[:], a1[:, c % 2], sg[:, c % 2], ALU.mult).then_inc(S["ds1_ready"], 1)
                pool.wait_ge(S["ds1_ready"], 2 * b + 1)
                g.tensor_tensor(ds1[:], sg[:, c % 2], ds1[:], ALU.subtract).then_inc(S["ds1_ready"], 1)
                pool.wait_ge(S["ds1_ready"], 2 * b + 2)
                wait(pool, "d1_ready", b - 1)
                g.tensor_tensor(ds[:, c % 2], a1[:, c % 2], ds1[:], ALU.add).then_inc(S["ds_ready"], 1)

            def keep_xnt(i, c):
                b = 2 * i + c
                pool.wait_ge(S["xnt_ready"], b + 1)
                g.tensor_copy(xnt_all[:, bass.ds(COLS * b, COLS)], xnt[:]).then_inc(S["copied"], 1)

            pool.wait_ge(S["consts_ready"], 1)
            rstd(0, 0)
            g.memset(centre[:], -1.0 / D).then_inc(S["consts_ready"], 1)
            pool.wait_ge(S["consts_ready"], 2)
            g.affine_select(out=centre[:], in_=centre[:], compare_op=ALU.not_equal, fill=1.0 - 1.0 / D, base=0,
                            pattern=[[-1, P]], channel_multiplier=1).then_inc(S["consts_ready"], 1)
            keep_xnt(0, 0)
            rstd(0, 1)
            silu_slope(0, 0)
            keep_xnt(0, 1)
            g.memset(upper[:], 1.0).then_inc(S["consts_ready"], 1)
            g.memset(ones[:], 1.0).then_inc(S["consts_ready"], 1)
            pool.wait_ge(S["consts_ready"], 5)
            g.affine_select(out=upper[:], in_=upper[:], compare_op=ALU.is_gt, fill=0.0, base=0,
                            pattern=[[1, P]], channel_multiplier=-1).then_inc(S["consts_ready"], 1)
            g.iota(rank[:].bitcast(I32), pattern=[[-1, E]], base=E, channel_multiplier=0
                   ).then_inc(S["consts_ready"], 1)
            g.iota(rows[:, :, C_ID:C_ID + 1].bitcast(I32), pattern=[[P, TILES], [0, 1]], base=0,
                   channel_multiplier=1).then_inc(S["rows_ids"], 1)
            with pool.Fori(0, NB // 2 - 1) as i:
                for c in (1, 2):
                    rstd(i, c + 1)
                    silu_slope(i, c)
                    keep_xnt(i, c + 1)
            silu_slope(0, NB - 1)

            pool.wait_ge(S["rows_ids"], 1)
            pool.wait_ge(S["disp_init"], 16 * E)
            for b in range(NB):
                pool.wait_ge(S["idx_ready"], b + 1)
                pool.wait_ge(S["mv2_ready"], 2 * (b + 1))
                for k in range(GROUP * b, GROUP * (b + 1)):
                    g.indirect_dma_start(
                        disp, bass.IndirectOffsetOnAxis(ap=idx[:, k:k + 1].bitcast(U32), axis=0),
                        rows[:, k, :], None, bounds_check=E * CAP - 1, oob_is_err=False
                    ).then_inc(S["scattered"], 16)

            def base_scales(h):
                n = TILES // 2
                k = slice(n * h, n * (h + 1))
                wait(pool, "rs2_ready", h)
                g.tensor_tensor(veps[:], rows[:, k, C_VAR], eps[:], ALU.add).then_inc(S["ve2_ready"], 1)
                pool.wait_ge(S["ve2_ready"], h + 1)
                g.tensor_tensor(rs2[:, k], veps[:], neg_half[:], ALU.pow).then_inc(S["rs2_ready"], 1)

            def rstd_rows(i, c):
                e = 2 * i + c
                pool.wait_ge(dr_loaded[c % 2], 16 * (i + c // 2 + 1))
                wait(pool, "rs3_ready", e)
                g.tensor_tensor(ve3[:], dr[:, bass.ds(e, 1), :, C_VAR].rearrange("p e s -> p (e s)"), eps[:, 0:ST], ALU.add).then_inc(S["ve3_ready"], 1)
                pool.wait_ge(S["ve3_ready"], e + 1)
                wait(pool, "dd_ready", e - 1)
                wait(pool, "tn_ready", e - 1)
                g.tensor_tensor(rs3[:, c % 2, :], ve3[:], neg_half[:, 0:ST], ALU.pow).then_inc(S["rs3_ready"], 1)

            def send(i, c):
                e = 2 * i + c
                pool.wait_ge(S["fin_ready"], e + 1)
                carry(c % 2 if c < 2 else 3 + c % 2)
                for s in range(ST):
                    g.indirect_dma_start(
                        out, bass.IndirectOffsetOnAxis(ap=ids[:, c % 2, s:s + 1].bitcast(U32), axis=0),
                        orow[:, c % 2, s, :], None, bounds_check=T - 1, oob_is_err=False
                    ).then_inc(sent[c % 2], 16)

            base_scales(0)
            rstd_rows(0, 0)
            base_scales(1)
            rstd_rows(0, 1)
            rstd_rows(0, 2)
            pool.wait_ge(base_stored[0], 16)
            pool.wait_ge(base_stored[1], 32)
            send(0, 0)
            rstd_rows(0, 3)
            send(0, 1)
            with pool.Fori(1, E // 2 - 1) as i:
                for c in (0, 1):
                    rstd_rows(i, c + 2)
                    send(i, c)
            send(0, E - 2)
            send(0, E - 1)

        @block.scalar
        def _(act):
            a = nc.scalar

            def turn_xn(i, c):
                b = 2 * i + c
                act.wait_ge(S["xt_done"], b + 1)
                wait(act, "err_done", b)
                wait(act, "copied", b)
                a.activation(xnt[:], bank[0][:], ACT.Copy, accum_out=xsum[:, bass.ds(b, 1)]
                             ).then_inc(S["xnt_ready"], 1)

            def sigmoid(i, c):
                b = 2 * i + c
                act.wait_ge(S["pre_done"], b + 1)
                wait(act, "ds_ready", b - 1)
                a.activation(sg[:, c % 2], bank[1][:], ACT.Sigmoid).then_inc(S["sig_ready"], 1)

            def turn_a1(i, c):
                b = 2 * i + c
                act.wait_ge(S["at_done"], b + 1)
                wait(act, "err_done", b)
                a.activation(a1t[:], bank[2][:], ACT.Copy).then_inc(S["a1t_ready"], 1)

            def turn_err(i, c):
                b = 2 * i + c
                act.wait_ge(S["et_done"], b + 1)
                wait(act, "dw_done", b)
                a.activation(ert[:], bank[4][:], ACT.Copy).then_inc(S["ert_ready"], 1)

            turn_xn(0, 0)
            sigmoid(0, 0)
            turn_a1(0, 0)
            turn_xn(0, 1)
            with act.Fori(0, NB // 2 - 1) as i:
                for c in (1, 2):
                    turn_err(i, c - 1)
                    sigmoid(i, c)
                    turn_a1(i, c)
                    turn_xn(i, c + 1)
            turn_err(0, NB - 2)
            sigmoid(0, NB - 1)
            act.wait_ge(S["gate_step"], 2)
            a.activation(gs[:], gp[:], ACT.Sigmoid).then_inc(S["gates_ready"], 1)
            turn_a1(0, NB - 1)
            turn_err(0, NB - 1)
            a.activation(warm[:, 0:1], gs[:, 0:1], ACT.Silu).then_inc(S["warmed"], 1)
            act.wait_ge(S["mz_mm"], 1)
            a.activation(n2[:], bank[5][:, 0:P], ACT.Copy).then_inc(S["n2_ready"], 1)

            def silu(i, c):
                b = 2 * i + c
                act.wait_ge(S["z_done"], b + 1)
                wait(act, "o_done", b)
                a.activation(st[:], bank[0][:], ACT.Silu).then_inc(S["silu_ready"], 1)

            def turn_x1(i, c):
                b = 2 * i + c
                act.wait_ge(S["x1t_done"], b + 1)
                wait(act, "lg_done", b)
                a.activation(x1t[:], bank[2][:], ACT.Copy).then_inc(S["x1t_ready"], 1)

            def base_rows(h):
                act.wait_ge(S["nm_ready"], 3)
                for k in range(TILES // 4 * h, TILES // 4 * (h + 1)):
                    ins = a.activation(tile(xr, k), rows[:, k, 0:D], ACT.Identity, bias=nmr2[:, k:k + 1],
                                       scale=rs2p[:, k:k + 1])
                ins.then_inc(S["base_ready"], 1)

            silu(0, 0)
            silu(0, 1)
            with act.Fori(0, NB // 2 - 1) as i:
                for c in (0, 1):
                    turn_x1(i, c)
                    silu(i, c + 2)
            turn_x1(0, NB - 2)
            turn_x1(0, NB - 1)

            def turn_t(i, c):
                e = 2 * i + c
                act.wait_ge(S["tt_mm"], e + 1)
                wait(act, "h_mm", 2 * FC * e)
                a.activation(tt[:, 0:4 * P], bank[6][:], ACT.Copy)
                a.activation(tt[:, 4 * P:], bank[7][:, 0:P], ACT.Copy).then_inc(S["tt_ready"], 1)

            def relu(i, c):
                e = 2 * i + c
                for k in range(2 * FC):
                    half, f = divmod(k, FC)
                    act.wait_ge(S["h_mm"], 2 * FC * e + k + 1)
                    if k == 0:
                        wait(act, "y_mm", e)
                    a.activation(ht[:, f, half * HALF:(half + 1) * HALF], bank[k % 4][:, 0:HALF], ACT.Relu
                                 ).then_inc(S["h_ready"], 1)

            def tanh(i, c):
                e = 2 * i + c
                act.wait_ge(S["dd_ready"], e + 1)
                wait(act, "rat_ready", e)
                a.activation(th[:], dd[:], ACT.Tanh, scale=0.5).then_inc(S["th_ready"], 1)

            base_rows(0)
            turn_t(0, 0)
            tanh(0, 0)
            relu(0, 0)
            base_rows(1)
            turn_t(0, 1)
            tanh(0, 1)
            relu(0, 1)
            turn_t(0, 2)
            with act.Fori(0, E // 2 - 2) as i:
                for c in (2, 3):
                    tanh(i, c)
                    relu(i, c)
                    turn_t(i, c + 1)
            tanh(0, E - 2)
            relu(0, E - 2)
            turn_t(0, E - 1)
            tanh(0, E - 1)
            relu(0, E - 1)

        @block.vector
        def _(dve):
            v = nc.vector

            def carry():
                v.memset(spare[:, 2:3], 0.0)

            def stats(i, c):
                b = 2 * i + c
                dve.wait_ge(x_loaded[c % 2], 16 * (i + c // 2 + 1))
                wait(dve, "mv_ready", b)
                carry()
                for k in range(GROUP):
                    ins = v.bn_stats(stat[:, k, :], xr[:, bass.ds(COLS * b + P * k, P)])
                ins.then_inc(S["mv_stat"], 1)
                dve.wait_ge(S["mv_stat"], b + 1)
                wait(dve, "xn_ready", b - 1)
                carry()
                for k in range(GROUP):
                    ins = v.bn_aggr(mv[:, c % 2, k, :], stat[:, k, :])
                ins.then_inc(S["mv_ready"], 1)

            def normalise(i, c):
                b = 2 * i + c
                dve.wait_ge(S["rstd_ready"], b + 1)
                wait(dve, "gt_done", b - 1)
                for k in range(GROUP):
                    ins = v.tensor_scalar(xn[:, c % 2, k * P:(k + 1) * P], xr[:, bass.ds(COLS * b + P * k, P)],
                                          mv[:, c % 2, k, 0:1], rs[:, c % 2, k:k + 1], ALU.subtract, ALU.mult)
                ins.then_inc(S["xn_ready"], 1)

            def make_a1(i, c):
                b = 2 * i + c
                dve.wait_ge(S["sig_ready"], b + 1)
                wait(dve, "g1_done", b - 1)
                wait(dve, "ds_ready", b - 1)
                v.tensor_tensor(a1[:, c % 2], bank[1][:], sg[:, c % 2], ALU.mult).then_inc(S["a1_ready"], 1)

            def make_d1(i, c):
                b = 2 * i + c
                dve.wait_ge(S["dw_done"], b + 1)
                dve.wait_ge(S["ds_ready"], b + 1)
                wait(dve, "gt_done", b)
                v.tensor_tensor(d1[:], bank[5][:], ds[:, c % 2], ALU.mult).then_inc(S["d1_ready"], 1)

            def clip_err(i, c):
                b = 2 * i + c
                dve.wait_ge(S["err_done"], b + 1)
                wait(dve, "g1_done", b)
                v.tensor_scalar(er[:], bank[3][:], ERR_CLIP, -ERR_CLIP, ALU.min, ALU.max
                                ).then_inc(S["clip_ready"], 1)

            stats(0, 0)
            v.memset(zeros[:], 0.0).then_inc(S["zeros_ready"], 1)
            normalise(0, 0)
            dve.wait_ge(S["wts_loaded"], 16)
            v.tensor_scalar(nwv[:], w(WVT), -1.0, None, ALU.mult).then_inc(S["setup_ready"], 1)
            dve.wait_ge(S["setup_mm"], 1)
            v.tensor_copy(a_w[:], bank[7][:, 0:P]).then_inc(S["setup_ready"], 1)
            stats(0, 1)
            make_a1(0, 0)
            normalise(0, 1)
            clip_err(0, 0)
            v.memset(empty[:], 0.0).then_inc(S["empty_ready"], 1)
            dve.wait_ge(S["empty_ready"], 1)
            v.memset(empty[:, :, C_ID:C_ID + 1].bitcast(I32), int(NO_TOKEN)).then_inc(S["empty_ready"], 1)
            dve.wait_ge(S["consts_ready"], 7)
            v.tensor_copy(rank[:], rank[:].bitcast(I32)).then_inc(S["dve_consts"], 1)
            v.memset(hot[:, 0, 0, :], 0.0).then_inc(S["dve_consts"], 1)
            dve.wait_ge(S["small_loaded"], 32)
            for k in range(3):
                v.tensor_copy(gate_w[:, k * P:(k + 1) * P], gw[:, k:k + 1].to_broadcast([P, P])
                              ).then_inc(S["dve_consts"], 1)
            dve.wait_ge(S["setup_mm"], 2)
            v.tensor_copy(wr_c[:], bank[7][:, 0:E]).then_inc(S["setup_ready"], 1)
            with dve.Fori(0, NB // 2 - 1) as i:
                for c in (1, 2):
                    stats(i, c + 1)
                    make_a1(i, c)
                    make_d1(i, c - 1)
                    normalise(i, c + 1)
                    clip_err(i, c)
            dve.wait_ge(S["gates_mm"], 1)
            v.reduce_sum(gl[:], bank[7][:, 0:3 * NB].rearrange("p (g b) -> p g b", g=3), AX
                         ).then_inc(S["gate_step"], 1)
            dve.wait_ge(S["gate_step"], 1)
            v.scalar_tensor_tensor(out=gp[:], in0=gl[:], scalar=1.0 / T, in1=gate_b[:], op0=ALU.mult,
                                   op1=ALU.add).then_inc(S["gate_step"], 1)
            make_a1(0, NB - 1)
            make_d1(0, NB - 2)
            dve.wait_ge(S["gates_ready"], 1)
            v.tensor_scalar(gk[:, 0:1], gs[:, 0:1], -1.0, 1.0, ALU.mult, ALU.add)
            v.tensor_scalar(gk[:, 1:2], gs[:, 1:2], -SCALE, None, ALU.mult)
            v.tensor_scalar(gk[:, 2:3], gs[:, 2:3], 0.0, None, ALU.mult).then_inc(S["upd_step"], 1)
            dve.wait_ge(S["upd_step"], 1)
            v.tensor_scalar(base0[:], w(W0T), gk[:, 0:1], gk[:, 2:3], ALU.mult, ALU.add)
            v.tensor_scalar(base1[:], w(W1N), gk[:, 0:1], gk[:, 2:3], ALU.mult, ALU.add
                            ).then_inc(S["upd_step"], 1)
            clip_err(0, NB - 1)
            make_d1(0, NB - 1)
            LIMIT = GRAD_CLIP / SCALE
            dve.wait_ge(S["gt_done"], NB)
            v.tensor_copy(gt[:], bank[6][:, P:2 * P]).then_inc(S["gt_ready"], 1)
            v.tensor_scalar(c1[:], bank[6][:, 0:P], LIMIT, -LIMIT, ALU.min, ALU.max).then_inc(S["upd_step"], 1)
            dve.wait_ge(S["upd_step"], 3)
            v.scalar_tensor_tensor(out=w1n[:], in0=c1[:], scalar=gk[:, 1:2], in1=base1[:], op0=ALU.mult,
                                   op1=ALU.add).then_inc(S["w1_ready"], 1)
            dve.wait_ge(S["g0_mm"], 1)
            v.tensor_scalar(c0[:], bank[7][:, 0:P], LIMIT, -LIMIT, ALU.min, ALU.max).then_inc(S["upd_step"], 1)
            dve.wait_ge(S["upd_step"], 4)
            v.scalar_tensor_tensor(out=w0n[:], in0=c0[:], scalar=gk[:, 1:2], in1=base0[:], op0=ALU.mult,
                                   op1=ALU.add).then_inc(S["w0_ready"], 1)
            dve.wait_ge(S["mz_mm"], 2)
            v.tensor_copy(mz[:], bank[7][:, 0:P]).then_inc(S["mz_ready"], 1)

            def add_x(i, c):
                b = 2 * i + c
                dve.wait_ge(S["o_done"], b + 1)
                v.tensor_tensor(rows[:, bass.ds(GROUP * b, GROUP), 0:D],
                                bank[1][:].rearrange("p (g d) -> p g d", d=P),
                                xr[:, bass.ds(COLS * b, COLS)].rearrange("p (g d) -> p g d", d=P), ALU.add
                                ).then_inc(S["x1_ready"], 1)

            def router(i, c):
                b = 2 * i + c
                lg = bank[3][:, 0:GROUP * E].rearrange("p (g e) -> p g e", e=E)
                ps = bank[4][:, 0:GROUP * E].rearrange("p (g e) -> p g e", e=E)
                d = rows[:, bass.ds(GROUP * b, GROUP), C_D:C_D + E]

                def wide(t):
                    return t[:].rearrange("p (g o) -> p g o", o=1).to_broadcast([P, GROUP, E])

                def s0():
                    dve.wait_ge(S["lg_done"], b + 1)
                    v.reduce_max(mx[:], lg, AX).then_inc(S["mx_ready"], 1)

                def s1():
                    dve.wait_ge(S["mx_ready"], b + 1)
                    v.tensor_tensor(d, lg, wide(mx), ALU.subtract).then_inc(S["d_ready"], 1)

                def s2():
                    dve.wait_ge(S["d_ready"], b + 1)
                    v.scalar_tensor_tensor(
                        out=cand[:], in0=d, scalar=0.0,
                        in1=rank[:].rearrange("p (o e) -> p o e", o=1).to_broadcast([P, GROUP, E]),
                        op0=ALU.is_ge, op1=ALU.mult).then_inc(S["cand_ready"], 1)

                def s3():
                    dve.wait_ge(S["cand_ready"], b + 1)
                    v.reduce_max(best[:], cand[:], AX).then_inc(S["best_ready"], 1)

                def s4():
                    dve.wait_ge(S["best_ready"], b + 1)
                    v.tensor_tensor(hot[:, c % 2, 1:, :], cand[:], wide(best), ALU.is_equal
                                    ).then_inc(S["hot_ready"], 1)

                def s5():
                    dve.wait_ge(S["hot_ready"], b + 1)
                    with nc.allow_low_precision("counts up to 32 are exact in bfloat16"):
                        v.reduce_sum(hot[:, 1 - c % 2, 0, :], hot[:, c % 2].rearrange("p g e -> p e g"), AX
                                     ).then_inc(S["count_ready"], 1)

                def s6():
                    dve.wait_ge(S["pos_mm"], b + 1)
                    v.tensor_tensor(own[:], ps, hot[:, c % 2, 1:, :], ALU.mult).then_inc(S["own_ready"], 1)

                def s7():
                    dve.wait_ge(S["own_ready"], b + 1)
                    v.reduce_sum(pos[:], own[:], AX).then_inc(S["pos_ready"], 1)

                def s8():
                    dve.wait_ge(S["pos_ready"], b + 1)
                    v.scalar_tensor_tensor(out=slot[:], in0=best[:], scalar=-float(CAP), in1=pos[:],
                                           op0=ALU.mult, op1=ALU.add).then_inc(S["slot_ready"], 1)
                    v.tensor_scalar(over[:], pos[:], float(CAP), NO_SLOT, ALU.is_ge, ALU.mult
                                    ).then_inc(S["over_ready"], 1)

                def s9():
                    dve.wait_ge(S["over_ready"], b + 1)
                    v.scalar_tensor_tensor(out=idx[:, bass.ds(GROUP * b, GROUP)], in0=slot[:],
                                           scalar=float(E * CAP), in1=over[:], op0=ALU.add, op1=ALU.add
                                           ).then_inc(S["idx_ready"], 1)

                return [s0, s1, s2, s3, s4, s5, s6, s7, s8, s9]

            def stats2(i, c):
                b = 2 * i + c

                def one(k):
                    def step():
                        if k == 0:
                            dve.wait_ge(S["x1_ready"], b + 1)
                            wait(dve, "mv2_ready", 2 * b)
                            carry()
                        ins = v.bn_stats(stat2[:, k, :], rows[:, bass.ds(GROUP * b + k, 1), 0:D
                                                              ].rearrange("p a d -> p (a d)"))
                        if k == GROUP - 1:
                            ins.then_inc(S["stat2_done"], 1)
                    return step

                def aggr(k):
                    def step():
                        if k == 0:
                            dve.wait_ge(S["stat2_done"], b + 1)
                            carry()
                        ins = v.bn_aggr(mv2[:, k, :], stat2[:, k, :])
                        if k == GROUP - 1:
                            ins.then_inc(S["mv2_ready"], 1)
                    return step

                def put():
                    dve.wait_ge(S["mv2_ready"], 2 * b + 1)
                    v.tensor_copy(rows[:, bass.ds(GROUP * b, GROUP), C_MEAN:C_VAR + 1], mv2[:]
                                  ).then_inc(S["mv2_ready"], 1)

                return [one(k) for k in range(GROUP)], [aggr(k) for k in range(GROUP)] + [put]

            def second(i, c, last=False):
                r = router(i, c - 1)
                s, g = stats2(i, c)
                for step in (r[0], s[0], r[1], s[1], r[2], s[2], r[3], s[3], r[4], g[0], r[5], g[1], r[6], g[2],
                             r[7], g[3], r[8], g[4], r[9]):
                    step()
                if not last:
                    add_x(i, c + 1)

            dve.wait_ge(S["dve_consts"], 5)
            add_x(0, 0)
            s, g = stats2(0, 0)
            for step in s + g:
                step()
            add_x(0, 1)
            with dve.Fori(0, NB // 2 - 1) as i:
                second(i, 1)
                second(i, 2)
            second(0, NB - 1, last=True)
            for step in router(0, NB - 1):
                step()

            def base_rows():
                for h in range(2):
                    k = slice(TILES // 2 * h, TILES // 2 * (h + 1))
                    dve.wait_ge(S["rs2_ready"], h + 1)
                    v.tensor_scalar(rs2p[:, k], rs2[:, k], 1.0, None, ALU.add).then_inc(S["nm_ready"], 1)
                    v.scalar_tensor_tensor(out=nmr2[:, k], in0=rs2[:, k], scalar=-1.0, in1=rows[:, k, C_MEAN],
                                           op0=ALU.mult, op1=ALU.mult).then_inc(S["nm_ready"], 2)
                    if h == 0:
                        norm_rows(0, 0)
                        scaled(0, 0)
                dve.wait_ge(S["nm_ready"], 6)
                for k in range(TILES // 2, TILES):
                    ins = v.tensor_scalar(tile(xr, k), rows[:, k, 0:D], rs2p[:, k:k + 1], nmr2[:, k:k + 1],
                                          ALU.mult, ALU.add)
                ins.then_inc(S["base_ready_v"], 1)

            def of(e, part):
                return dr[:, bass.ds(e, 1), :, part].rearrange("p e s c -> p (e s) c")

            def norm_rows(i, c):
                e = 2 * i + c
                dve.wait_ge(S["rs3_ready"], e + 1)
                wait(dve, "tt_mm", e)
                row = of(e, slice(0, ROW))
                for s in range(ST):
                    ins = v.tensor_scalar(tn[:, s * P:(s + 1) * P], row[:, s, 0:D], row[:, s, C_MEAN:C_MEAN + 1],
                                          rs3[:, c % 2, s:s + 1], ALU.subtract, ALU.mult)
                ins.then_inc(S["tn_ready"], 1)

            def scaled(i, c):
                e = 2 * i + c
                wait(dve, "th_ready", e)
                v.tensor_tensor(dd[:], of(e, slice(C_D, C_D + E)),
                                rs3[:, c % 2].rearrange("p (s o) -> p s o", o=1).to_broadcast([P, ST, E]),
                                ALU.mult).then_inc(S["dd_ready"], 1)

            def pmax(i, c):
                e = 2 * i + c
                dve.wait_ge(S["th_ready"], e + 1)
                v.tensor_scalar(den[:], th[:], -1.0, 1.0, ALU.mult, ALU.add).then_inc(S["den_ready"], 1)
                dve.wait_ge(S["den_ready"], e + 1)
                v.reciprocal(rat[:], den[:]).then_inc(S["rat_ready"], 1)
                dve.wait_ge(S["rat_ready"], e + 1)
                v.scalar_tensor_tensor(out=den[:], in0=th[:], scalar=1.0, in1=rat[:], op0=ALU.add,
                                       op1=ALU.mult).then_inc(S["esum_ready"], 1)
                dve.wait_ge(S["esum_ready"], 2 * e + 1)
                v.reduce_sum(esum[:], den[:], AX).then_inc(S["esum_ready"], 1)
                dve.wait_ge(S["esum_ready"], 2 * e + 2)
                v.reciprocal(pm[:], esum[:]).then_inc(S["pm_ready"], 1)

            def finish(i, c, first):
                e = 2 * i + c
                if not first:
                    dve.wait_ge(sent[c % 2], 16 * ST * (i + c // 2))
                v.tensor_copy(ids[:, c % 2].rearrange("p (s o) -> p s o", o=1),
                              of(e, slice(C_ID, C_ID + 1)).bitcast(I32))
                dve.wait_ge(S["y_mm"], e + 1)
                dve.wait_ge(S["pm_ready"], e + 1)
                row = of(e, slice(0, ROW))
                for s in range(ST):
                    y = bank[4][:, s * P:(s + 1) * P] if s < 4 else bank[5][:, 0:P]
                    ins = v.scalar_tensor_tensor(out=orow[:, c % 2, s, :], in0=y, scalar=pm[:, s:s + 1],
                                                 in1=row[:, s, 0:D], op0=ALU.mult, op1=ALU.add)
                ins.then_inc(S["fin_ready"], 1)

            def expert(i, c, first=False, last=False):
                if not last:
                    norm_rows(i, c + 1)
                pmax(i, c)
                if not last:
                    scaled(i, c + 1)
                finish(i, c, first)

            base_rows()
            expert(0, 0, first=True)
            expert(0, 1, first=True)
            with dve.Fori(0, E // 2 - 2) as i:
                expert(i, 2)
                expert(i, 3)
            expert(0, E - 2)
            expert(0, E - 1, last=True)

        @block.tensor
        def _(pe):
            t = nc.tensor

            def turn(dst, src, n=GROUP):
                for k in range(n):
                    ins = t.transpose(tile(dst, k), tile(src, k), ident[:])
                return ins

            def turn_xn(i, c):
                b = 2 * i + c
                pe.wait_ge(S["xn_ready"], b + 1)
                wait(pe, "xnt_ready", b)
                turn(bank[0], xn[:, c % 2]).then_inc(S["xt_done"], 1)

            def pre(i, c):
                b = 2 * i + c
                pe.wait_ge(S["xnt_ready"], b + 1)
                wait(pe, "a1_ready", b)
                for k in range(GROUP):
                    ins = t.matmul(tile(bank[1], k), tile(xnt, k), a_w[:], start=True, stop=True)
                ins.then_inc(S["pre_done"], 1)

            def turn_a1(i, c):
                b = 2 * i + c
                pe.wait_ge(S["a1_ready"], b + 1)
                wait(pe, "a1t_ready", b)
                turn(bank[2], a1[:, c % 2]).then_inc(S["at_done"], 1)

            def err(i, c):
                b = 2 * i + c
                pe.wait_ge(S["a1t_ready"], b + 1)
                wait(pe, "clip_ready", b)
                for k in range(GROUP):
                    t.matmul(tile(bank[3], k), tile(a1t, k), w(W1T), start=True, stop=False)
                    ins = t.matmul(tile(bank[3], k), tile(xnt, k), nwv[:], start=False, stop=True)
                ins.then_inc(S["err_done"], 1)

            def turn_err(i, c):
                b = 2 * i + c
                pe.wait_ge(S["clip_ready"], b + 1)
                wait(pe, "ert_ready", b)
                turn(bank[4], er).then_inc(S["et_done"], 1)

            def back(i, c):
                b = 2 * i + c
                pe.wait_ge(S["ert_ready"], b + 1)
                wait(pe, "d1_ready", b)
                for k in range(GROUP):
                    ins = t.matmul(tile(bank[5], k), tile(ert, k), w(W1N), start=True, stop=True)
                ins.then_inc(S["dw_done"], 1)

            def grad1(i, c):
                for k in range(GROUP):
                    ins = t.matmul(bank[6][:, 0:P], tile(er, k), tile(a1[:, c % 2], k), start=False, stop=False,
                                   skip_group_check=True)
                ins.then_inc(S["g1_done"], 1)

            def grad0(i, c):
                pe.wait_ge(S["d1_ready"], 2 * i + c + 1)
                for k in range(GROUP):
                    ins = t.matmul(bank[6][:, P:2 * P], tile(xn[:, c % 2], k), tile(d1, k), start=False,
                                   stop=False, skip_group_check=True)
                ins.then_inc(S["gt_done"], 1)

            pe.wait_ge(S["zeros_ready"], 1)
            t.matmul(bank[6][:, 0:2 * P], zeros[:, 0:P], zeros[:], start=True, stop=True)
            pe.wait_ge(S["ident_ready"], 2)
            turn_xn(0, 0)
            pe.wait_ge(S["wts_loaded"], 16)
            t.matmul(bank[7][:, 0:P], w(WK), w(W0T), start=True, stop=True).then_inc(S["setup_mm"], 1)
            pe.wait_ge(S["setup_ready"], 2)
            pre(0, 0)
            turn_a1(0, 0)
            err(0, 0)
            turn_xn(0, 1)
            pe.wait_ge(S["consts_ready"], 3)
            pe.wait_ge(S["small_loaded"], 32)
            t.matmul(bank[7][:, 0:E], centre[:], gw[:, 3:3 + E], start=True, stop=True
                     ).then_inc(S["setup_mm"], 1)
            with pe.Fori(0, NB // 2 - 1) as i:
                for c in (1, 2):
                    turn_err(i, c - 1)
                    pre(i, c)
                    back(i, c - 1)
                    grad1(i, c - 1)
                    turn_a1(i, c)
                    grad0(i, c - 1)
                    err(i, c)
                    turn_xn(i, c + 1)
            turn_err(0, NB - 2)
            pre(0, NB - 1)
            pe.wait_ge(S["setup_ready"], 3)
            pe.wait_ge(S["dve_consts"], 5)
            for k in range(3):
                ins = t.matmul(bank[7][:, k * NB:(k + 1) * NB], tile(gate_w, k), xsum[:], start=True, stop=True)
            ins.then_inc(S["gates_mm"], 1)
            back(0, NB - 2)
            grad1(0, NB - 2)
            turn_a1(0, NB - 1)
            grad0(0, NB - 2)
            err(0, NB - 1)
            turn_err(0, NB - 1)
            back(0, NB - 1)
            grad1(0, NB - 1)
            grad0(0, NB - 1)
            pe.wait_ge(S["gt_ready"], 1)
            t.matmul(bank[7][:, 0:P], w(WKT), gt[:], start=True, stop=True).then_inc(S["g0_mm"], 1)
            pe.wait_ge(S["w1_ready"], 1)
            t.matmul(bank[5][:, 0:P], w1n[:], w(WOT), start=True, stop=True).then_inc(S["mz_mm"], 1)
            pe.wait_ge(S["w0_ready"], 1)
            t.matmul(bank[7][:, 0:P], w(WQ), w0n[:], start=True, stop=True).then_inc(S["mz_mm"], 1)

            def hidden(i, c):
                b = 2 * i + c
                wait(pe, "silu_ready", b)
                t.matmul(bank[0][:], mz[:], xnt_all[:, bass.ds(COLS * b, COLS)], start=True, stop=True
                         ).then_inc(S["z_done"], 1)

            def output(i, c):
                b = 2 * i + c
                pe.wait_ge(S["silu_ready"], b + 1)
                wait(pe, "x1_ready", b)
                for k in range(GROUP):
                    ins = t.matmul(tile(bank[1], k), tile(st, k), n2[:], start=True, stop=True)
                ins.then_inc(S["o_done"], 1)

            def turn_x1(i, c):
                b = 2 * i + c
                pe.wait_ge(S["x1_ready"], b + 1)
                wait(pe, "x1t_ready", b)
                for k in range(GROUP):
                    ins = t.transpose(tile(bank[2], k), x1_tile(i, c, k), ident[:])
                ins.then_inc(S["x1t_done"], 1)

            def x1_tile(i, c, k):
                return rows[:, GROUP * (2 * i + c) + k, 0:D]

            def logits(i, c):
                b = 2 * i + c
                pe.wait_ge(S["x1t_ready"], b + 1)
                wait(pe, "d_ready", b)
                for k in range(GROUP):
                    ins = t.matmul(bank[3][:, k * E:(k + 1) * E], tile(x1t, k), wr_c[:], start=True, stop=True)
                ins.then_inc(S["lg_done"], 1)

            def positions(i, c):
                b = 2 * i + c
                pe.wait_ge(S["hot_ready"], b + 1)
                wait(pe, "count_ready", b)
                wait(pe, "own_ready", b)
                ps = bank[4][:, 0:GROUP * E]
                h = hot[:, c % 2]
                t.matmul(ps, upper[:], h[:, 1:, :].rearrange("p g e -> p (g e)"), start=True, stop=False)
                for k in range(GROUP):
                    n = GROUP - k
                    ins = t.matmul(ps[:, k * E:].rearrange("p (g e) -> p g e", e=E), ones[:],
                                   h[:, k:k + 1, :].to_broadcast([P, n, E]), start=False,
                                   stop=(k == GROUP - 1))
                ins.then_inc(S["pos_mm"], 1)

            pe.wait_ge(S["mz_ready"], 1)
            hidden(0, 0)
            pe.wait_ge(S["n2_ready"], 1)
            output(0, 0)
            hidden(0, 1)
            pe.wait_ge(S["consts_ready"], 6)
            for b in range(NB):
                turn_x1(0, b)
                if b + 1 < NB:
                    output(0, b + 1)
                if b:
                    positions(0, b - 1)
                logits(0, b)
                if b + 2 < NB:
                    hidden(0, b + 2)
            positions(0, NB - 1)

            def turn_t(i, c):
                e = 2 * i + c
                pe.wait_ge(S["tn_ready"], e + 1)
                wait(pe, "tt_ready", e)
                for s in range(ST):
                    o = tile(bank[6], s) if s < 4 else bank[7][:, 0:P]
                    ins = t.transpose(o, tile(tn, s), ident[:])
                ins.then_inc(S["tt_mm"], 1)

            def layer1(i, c):
                e = 2 * i + c
                pe.wait_ge(S["tt_ready"], e + 1)
                pe.wait_ge(w1_loaded[c % 2], 16 * (i + c // 2 + 1))
                for k in range(2 * FC):
                    half, f = divmod(k, FC)
                    if k >= 4:
                        pe.wait_ge(S["h_ready"], 2 * FC * e + k - 3)
                    t.matmul(bank[k % 4][:, 0:HALF], w1r[:, c % 2, f * P:(f + 1) * P],
                             tt[:, half * HALF:(half + 1) * HALF], start=True, stop=True
                             ).then_inc(S["h_mm"], 1)

            def layer2(i, c):
                e = 2 * i + c
                pe.wait_ge(S["h_ready"], 2 * FC * (e + 1))
                pe.wait_ge(w2_loaded[c % 2], 16 * (i + c // 2 + 1))
                wait(pe, "fin_ready", e)
                for s in range(ST):
                    y = tile(bank[4], s) if s < 4 else bank[5][:, 0:P]
                    for f in range(FC):
                        ins = t.matmul(y, ht[:, f, s * P:(s + 1) * P], w2r[:, c % 2, f, :],
                                       start=(f == 0), stop=(f == FC - 1))
                ins.then_inc(S["y_mm"], 1)

            turn_t(0, 0)
            with pe.Fori(0, E // 2 - 1) as i:
                for c in (0, 1):
                    layer1(i, c)
                    turn_t(i, c + 1)
                    layer2(i, c)
            layer1(0, E - 2)
            turn_t(0, E - 1)
            layer2(0, E - 2)
            layer1(0, E - 1)
            layer2(0, E - 1)


def kernel(**inputs):
    import concourse.bacc as bacc
    from concourse.bass_utils import run_bass_kernel_spmd

    a = {k.removeprefix("L0_"): np.asarray(v) for k, v in inputs.items()}
    x = a["attn_x"]
    Wk, Wv, Wq, Wout, W0, W1 = (a["attn_" + n] for n in ("Wk", "Wv", "Wq", "Wout", "W0", "W1"))
    arrays = {
        "x": np.ascontiguousarray(x.reshape(-1, x.shape[-1])),
        "wpack": np.ascontiguousarray(np.concatenate([Wk, Wk.T, Wv.T, Wq, W0.T, W1, W1.T, Wout.T], axis=1)),
        "wsmall": np.ascontiguousarray(np.concatenate(
            [a["attn_Wg_decay"].T, a["attn_Wg_lr"].T, a["attn_Wg_mom"].T, a["ffn_Wr"]], axis=1)),
        "biases": np.concatenate([a["attn_bg_decay"], a["attn_bg_lr"], a["attn_bg_mom"]])[None, :],
        "w_up": np.ascontiguousarray(a["ffn_W1"]),
        "w_down": np.ascontiguousarray(a["ffn_W2"]),
    }
    nc = bacc.Bacc("TRN2", target_bir_lowering=False, num_devices=1)
    args = [nc.dram_tensor(f"in_{n}", v.shape, mybir.dt.from_np(v.dtype), kind="ExternalInput").ap()
            for n, v in arrays.items()]
    y = nc.dram_tensor("out_y", arrays["x"].shape, F32, kind="ExternalOutput").ap()
    build(nc, *args, y)
    r = run_bass_kernel_spmd(nc, [{f"in_{n}": v for n, v in arrays.items()}], core_ids=[0])
    return r.results[0]["out_y"].reshape(x.shape)
```

```python
from contextlib import ExitStack

import numpy as np

import concourse.bass as bass
from concourse import mybir

ALU = mybir.AluOpType
ACT = mybir.ActivationFunctionType
F32 = mybir.dt.float32
BF16 = mybir.dt.bfloat16
F32R = mybir.dt.float32r
I32 = mybir.dt.int32
U32 = mybir.dt.uint32
AX = mybir.AxisListType.X

P = 128
EPS = 1e-5
ERR_CLIP = 5.0
GRAD_CLIP = 1.0
SCALE = 2.0 / 512.0
CAP_FACTOR = 1.25
GROUP = 4
WK, WKT, WVT, WQ, W0T, W1N, W1T, WOT = range(8)


def build(nc: bass.Bass, x: bass.AP, wpack: bass.AP, wsmall: bass.AP, biases: bass.AP,
          w_up: bass.AP, w_down: bass.AP, out: bass.AP):
    T, D = x.shape
    E, _, F = w_up.shape
    assert D == P
    TILES = T // P
    NB = TILES // GROUP
    COLS = GROUP * P
    CAP = int(CAP_FACTOR * T / E)
    ST = CAP // P
    HALF = CAP // 2
    FC = F // P
    BT = TILES // 4
    assert NB == 8 and E == 8 and CAP == ST * P and HALF <= 512 and FC == 4
    C_MEAN, C_VAR, C_D, C_ID = D, D + 1, D + 2, D + 2 + E
    ROW = C_ID + 1
    NO_SLOT = float(2 ** 20)
    NO_TOKEN = float(T)

    disp = nc.dram_tensor("disp", [E * CAP, ROW], F32, kind="Internal").ap()

    with ExitStack() as ctx:
        def sb(name, shape, dt=F32):
            return ctx.enter_context(nc.sbuf_tensor(name, shape, dt))

        def sem(name):
            return ctx.enter_context(nc.semaphore(name))

        bank = [ctx.enter_context(nc.psum_tensor(f"bank{i}", [P, 512], F32)) for i in range(8)]

        ident = sb("ident", [P, P])
        centre = sb("centre", [P, P])
        upper = sb("upper", [P, P], BF16)
        ones = sb("ones", [P, P], BF16)
        zeros = sb("zeros", [P, 2 * P])
        neg_half = sb("neg_half", [P, TILES // 2])
        eps = sb("eps", [P, TILES // 2])
        rank = sb("rank", [P, E])
        wts = sb("wts", [P, 8 * P])
        gw = sb("gw", [P, 3 + E])
        gate_w = sb("gate_w", [P, 3 * P])
        gate_b = sb("gate_b", [P, 3])
        a_w = sb("a_w", [P, P])
        nwv = sb("nwv", [P, P])
        wr_c = sb("wr_c", [P, E])
        xr = sb("xr", [P, TILES * P])
        stat = sb("stat", [P, GROUP, 6])
        mv = sb("mv", [P, 2, GROUP, 2])
        veps = sb("veps", [P, TILES // 2])
        rs = sb("rs", [P, 2, GROUP])
        xn = sb("xn", [P, 2, COLS])
        xnt = sb("xnt", [P, COLS])
        xnt_all = sb("xnt_all", [P, T])
        xsum = sb("xsum", [P, NB])
        sg = sb("sg", [P, 2, COLS])
        a1 = sb("a1", [P, 2, COLS])
        one_less = sb("one_less", [P, COLS])
        ds1 = sb("ds1", [P, COLS])
        ds = sb("ds", [P, 2, COLS])
        a1t = sb("a1t", [P, COLS])
        er = sb("er", [P, COLS])
        ert = sb("ert", [P, COLS])
        d1 = sb("d1", [P, COLS])
        gl = sb("gl", [P, 3])
        gp = sb("gp", [P, 3])
        gs = sb("gs", [P, 3])
        gk = sb("gk", [P, 3])
        base0 = sb("base0", [P, P])
        base1 = sb("base1", [P, P])
        gt = sb("gt", [P, P])
        c0 = sb("c0", [P, P])
        c1 = sb("c1", [P, P])
        w0n = sb("w0n", [P, P])
        w1n = sb("w1n", [P, P])
        mz = sb("mz", [P, P])
        n2 = sb("n2", [P, P])
        st = sb("st", [P, COLS])
        rows = sb("rows", [P, TILES, ROW])
        stat2 = sb("stat2", [P, GROUP, 6])
        mv2 = sb("mv2", [P, GROUP, 2])
        x1t = sb("x1t", [P, COLS])
        mx = sb("mx", [P, GROUP])
        cand = sb("cand", [P, GROUP, E])
        best = sb("best", [P, GROUP])
        hot = sb("hot", [P, 2, GROUP + 1, E], BF16)
        own = sb("own", [P, GROUP, E])
        pos = sb("pos", [P, GROUP])
        slot = sb("slot", [P, GROUP])
        over = sb("over", [P, GROUP])
        idx = sb("idx", [P, TILES], I32)
        rs2 = sb("rs2", [P, TILES])
        rs2p = sb("rs2p", [P, TILES])
        nmr2 = sb("nmr2", [P, TILES])
        empty = sb("empty", [P, ST, ROW])
        dr = sb("dr", [P, E, ST, ROW])
        w1_in = dr[:].rearrange("p e s c -> p (e s c)")[:, 0:E * F]
        ids = sb("ids", [P, 2, ST], I32)
        ve3 = sb("ve3", [P, ST])
        rs3 = sb("rs3", [P, 2, ST])
        tt_hi = sb("tt_hi", [P, CAP])
        tt_lo = sb("tt_lo", [P, CAP])
        dd = sb("dd", [P, ST, E])
        th = sb("th", [P, ST, E])
        den = sb("den", [P, ST, E])
        rat = sb("rat", [P, ST, E])
        esum = sb("esum", [P, ST])
        pm = sb("pm", [P, ST])
        yscale = sb("yscale", [P, ST])
        w1_hi = sb("w1_hi", [P, E, F])
        w1_lo = sb("w1_lo", [P, E, F])
        w2 = sb("w2", [P, E, FC, P])
        ht = sb("ht", [P, FC, CAP])
        orow = sb("orow", [P, 2, ST, P])
        warm = sb("warm", [P, 2])
        spare = sb("spare", [P, 5])

        def w(k):
            return wts[:, k * P:(k + 1) * P]

        def err_bank(h):
            return bank[(3, 7)[h]]

        def turned_half(h):
            return bank[(4, 2)[h]][:, 0:2 * P]

        def back_of_half(h):
            return bank[(5, 1)[h]][:, 0:2 * P]

        def centre_bank(e):
            return bank[(0, 5, 6, 7)[e % 4]][:]

        def y_tile(s):
            o = bank[(4, 5, 3)[s // 2]][:, s % 2 * P:(s % 2 + 1) * P]
            return o, min(s | 1, ST - 1)

        def f32r(ap):
            return ap.bitcast(F32R)

        def tile(t, g):
            return t[:, g * P:(g + 1) * P]

        names = """wts_loaded small_loaded ident_ready consts_ready zeros_ready dve_consts empty_ready disp_init
            mv_stat mv_ready veps_ready rstd_ready xn_ready xt_done xnt_ready copied pre_done sig_ready one_less_ready a1_ready
            at_done a1t_ready err_done clip_ready et_done ert_ready dw_done ds1_ready ds_ready d1_ready g1_done
            gt_done setup_mm setup_ready gates_mm gate_step gates_ready upd_step gt_ready g0_mm w0_ready w1_ready
            mz_mm mz_ready n2_ready z_done silu_ready o_done x1_ready x1t_done x1t_ready lg_done
            mx_ready d_ready cand_ready best_ready hot_ready count_ready pos_mm own_ready pos_ready slot_ready
            over_ready idx_ready stat2_done mv2_ready scattered ve2_ready rs2_ready nm_ready base_ready base_ready_v
            rows_ids ve3_ready rs3_ready w_up_loaded w_down_loaded centred hi_ready lo_ready tt_mm tt_hi_ready
            tt_lo_ready h_mm h_ready y_mm base_stored yscale_ready
            dd_ready th_ready den_ready rat_ready esum_ready pm_ready fin_ready warmed""".split()
        S = {n: sem(n) for n in names}
        x_loaded = [sem(f"x_loaded{i}") for i in range(2)]
        dr_loaded = [sem(f"dr_loaded{i}") for i in range(2)]
        sent = [sem(f"sent{i}") for i in range(2)]

        def wait(eng, s, count):
            if isinstance(count, int) and count <= 0:
                return
            eng.wait_ge(S[s] if isinstance(s, str) else s, count)


        block = ctx.enter_context(nc.Block())

        @block.sync
        def _(sp):
            def load_x(i, c):
                if isinstance(i, int) and c < 2:
                    pass
                else:
                    sp.wait_ge(x_loaded[c % 2], 16 * (i + c // 2))
                b = 2 * i + c
                sp.dma_start(xr[:, bass.ds(COLS * b, COLS)].rearrange("p (g d) -> p g d", d=P),
                             x_view[:, bass.ds(GROUP * b, GROUP), :]).then_inc(x_loaded[c % 2], 16)

            x_view = x.rearrange("(n p) d -> p n d", p=P)
            out_view = out.rearrange("(n p) d -> p n d", p=P)
            load_x(0, 0)
            load_x(0, 1)
            sp.dma_start(wts[:], wpack).then_inc(S["wts_loaded"], 16)
            sp.dma_start(gw[:], wsmall).then_inc(S["small_loaded"], 16)
            sp.dma_start(gate_b[:], biases.to_broadcast([P, 3])).then_inc(S["small_loaded"], 16)
            with sp.Fori(0, NB // 2 - 1) as i:
                load_x(i, 2)
                load_x(i, 3)
            sp.dma_start(w1_in.rearrange("p (e f) -> p e f", f=F), w_up.rearrange("e d f -> d e f")).then_inc(S["w_up_loaded"], 16)
            sp.dma_start(w2[:], w_down.rearrange("e (c p) d -> p e c d", p=P)).then_inc(S["w_down_loaded"], 16)
            sp.wait_ge(S["empty_ready"], 2)
            with sp.Fori(0, E) as e:
                sp.dma_start(disp[bass.ds(CAP * e, CAP), :].rearrange("(p s) c -> p s c", s=ST),
                             empty[:]).then_inc(S["disp_init"], 16)

            def load_rows(i, c):
                if not (isinstance(i, int) and c < 2):
                    sp.wait_ge(dr_loaded[c % 2], 16 * (i + c // 2))
                e = 2 * i + c
                sp.dma_start(dr[:, bass.ds(e, 1)].rearrange("p e s c -> p (e s c)"),
                             disp[bass.ds(CAP * e, CAP), :].rearrange("(p s) c -> p (s c)", s=ST)
                             ).then_inc(dr_loaded[c % 2], 16)

            sp.wait_ge(S["centred"], E)
            sp.wait_ge(S["scattered"], 16 * TILES)
            def store_base(q, made, count):
                k0 = BT * q
                sp.wait_ge(S[made], count)
                sp.dma_start(out_view[:, k0:k0 + BT, :],
                             xr[:, k0 * P:(k0 + BT) * P].rearrange("p (g d) -> p g d", d=P)
                             ).then_inc(S["base_stored"], 16)

            for e in range(3):
                load_rows(0, e)
            store_base(0, "base_ready_v", 1)
            load_rows(0, 3)
            store_base(1, "base_ready_v", 2)
            store_base(2, "base_ready_v", 3)
            store_base(3, "base_ready", 1)
            with sp.Fori(1, E // 2 - 1) as i:
                load_rows(i, 2)
                load_rows(i, 3)
            sp.wait_ge(S["base_stored"], 16 * 4)
            sp.wait_ge(sent[0], 16 * ST * E // 2)
            sp.wait_ge(sent[1], 16 * ST * E // 2)

        @block.gpsimd
        def _(pool):
            g = nc.gpsimd

            def carry(k):
                g.tensor_tensor(spare[:, k:k + 1], eps[:, 0:1], eps[:, 0:1], ALU.add)

            g.memset(ident[:], 0.0).then_inc(S["ident_ready"], 1)
            pool.wait_ge(S["ident_ready"], 1)
            g.affine_select(out=ident[:], in_=ident[:], compare_op=ALU.not_equal, fill=1.0, base=0,
                            pattern=[[-1, P]], channel_multiplier=1).then_inc(S["ident_ready"], 1)
            g.memset(eps[:], EPS)
            g.memset(neg_half[:], -0.5).then_inc(S["consts_ready"], 1)

            def rstd(i, c):
                b = 2 * i + c
                wait(pool, "rstd_ready", b)
                pool.wait_ge(S["mv_ready"], b + 1)
                g.tensor_tensor(veps[:, 0:GROUP], mv[:, c % 2, :, 1], eps[:, 0:GROUP], ALU.add
                                ).then_inc(S["veps_ready"], 1)
                wait(pool, "xn_ready", b - 1)
                pool.wait_ge(S["veps_ready"], b + 1)
                g.tensor_tensor(rs[:, c % 2, :], veps[:, 0:GROUP], neg_half[:, 0:GROUP], ALU.pow
                                ).then_inc(S["rstd_ready"], 1)

            def silu_slope(i, c):
                b = 2 * i + c
                pool.wait_ge(S["a1_ready"], 2 * b + 2)
                wait(pool, "ds_ready", b)
                pool.wait_ge(S["one_less_ready"], b + 1)
                g.tensor_tensor(ds1[:], a1[:, c % 2], one_less[:], ALU.mult).then_inc(S["ds1_ready"], 1)
                wait(pool, "d1_ready", b - 1)
                pool.wait_ge(S["ds1_ready"], b + 1)
                g.tensor_tensor(ds[:, c % 2], sg[:, c % 2], ds1[:], ALU.add).then_inc(S["ds_ready"], 1)

            def keep_xnt(i, c):
                b = 2 * i + c
                pool.wait_ge(S["xnt_ready"], b + 1)
                g.tensor_copy(xnt_all[:, bass.ds(COLS * b, COLS)], xnt[:]).then_inc(S["copied"], 1)

            g.memset(centre[:], -1.0 / D).then_inc(S["consts_ready"], 1)
            pool.wait_ge(S["consts_ready"], 2)
            g.affine_select(out=centre[:], in_=centre[:], compare_op=ALU.not_equal, fill=1.0 - 1.0 / D, base=0,
                            pattern=[[-1, P]], channel_multiplier=1).then_inc(S["consts_ready"], 1)
            rstd(0, 0)
            rstd(0, 1)
            keep_xnt(0, 0)
            silu_slope(0, 0)
            keep_xnt(0, 1)
            g.memset(upper[:], 1.0).then_inc(S["consts_ready"], 1)
            g.memset(ones[:], 1.0).then_inc(S["consts_ready"], 1)
            pool.wait_ge(S["consts_ready"], 5)
            g.affine_select(out=upper[:], in_=upper[:], compare_op=ALU.is_gt, fill=0.0, base=0,
                            pattern=[[1, P]], channel_multiplier=-1).then_inc(S["consts_ready"], 1)
            g.iota(rank[:].bitcast(I32), pattern=[[-1, E]], base=E, channel_multiplier=0
                   ).then_inc(S["consts_ready"], 1)
            g.iota(rows[:, :, C_ID:C_ID + 1].bitcast(I32), pattern=[[P, TILES], [0, 1]], base=0,
                   channel_multiplier=1).then_inc(S["rows_ids"], 1)
            with pool.Fori(0, NB // 2 - 1) as i:
                for c in (1, 2):
                    rstd(i, c + 1)
                    silu_slope(i, c)
                    keep_xnt(i, c + 1)
            silu_slope(0, NB - 1)

            pool.wait_ge(S["rows_ids"], 1)
            pool.wait_ge(S["disp_init"], 16 * E)
            for b in range(NB):
                pool.wait_ge(S["idx_ready"], b + 1)
                pool.wait_ge(S["mv2_ready"], 2 * (b + 1))
                for k in range(GROUP * b, GROUP * (b + 1)):
                    g.indirect_dma_start(
                        disp, bass.IndirectOffsetOnAxis(ap=idx[:, k:k + 1].bitcast(U32), axis=0),
                        rows[:, k, :], None, bounds_check=E * CAP - 1, oob_is_err=False
                    ).then_inc(S["scattered"], 16)

            def base_scales(h):
                n = TILES // 2
                k = slice(n * h, n * (h + 1))
                wait(pool, "rs2_ready", h)
                g.tensor_tensor(veps[:], rows[:, k, C_VAR], eps[:], ALU.add).then_inc(S["ve2_ready"], 1)
                pool.wait_ge(S["ve2_ready"], h + 1)
                g.tensor_tensor(rs2[:, k], veps[:], neg_half[:], ALU.pow).then_inc(S["rs2_ready"], 1)

            def rstd_rows(i, c):
                e = 2 * i + c
                pool.wait_ge(dr_loaded[c % 2], 16 * (i + c // 2 + 1))
                wait(pool, "rs3_ready", e)
                g.tensor_tensor(ve3[:], dr[:, bass.ds(e, 1), :, C_VAR].rearrange("p e s -> p (e s)"), eps[:, 0:ST], ALU.add).then_inc(S["ve3_ready"], 1)
                wait(pool, "yscale_ready", e - 1)
                pool.wait_ge(S["ve3_ready"], e + 1)
                g.tensor_tensor(rs3[:, c % 2, :], ve3[:], neg_half[:, 0:ST], ALU.pow).then_inc(S["rs3_ready"], 1)

            def send_tile(c, s):
                g.indirect_dma_start(
                    out, bass.IndirectOffsetOnAxis(ap=ids[:, c % 2, s:s + 1].bitcast(U32), axis=0),
                    orow[:, c % 2, s, :], None, bounds_check=T - 1, oob_is_err=False
                ).then_inc(sent[c % 2], 16)

            def send(i, c):
                pool.wait_ge(S["fin_ready"], ST * (2 * i + c + 1))
                carry(c % 2 if c < 2 else 3)
                for s in range(ST):
                    send_tile(c, s)

            base_scales(0)
            base_scales(1)
            rstd_rows(0, 0)
            rstd_rows(0, 1)
            rstd_rows(0, 2)
            pool.wait_ge(S["base_stored"], 16 * 4)
            send(0, 0)
            rstd_rows(0, 3)
            send(0, 1)
            with pool.Fori(1, E // 2 - 1) as i:
                for c in (0, 1):
                    rstd_rows(i, c + 2)
                    send(i, c)
            send(0, E - 2)
            for s in range(ST):
                pool.wait_ge(S["fin_ready"], ST * (E - 1) + s + 1)
                send_tile(E - 1, s)

        @block.scalar
        def _(act):
            a = nc.scalar

            def turn_xn(i, c):
                b = 2 * i + c
                wait(act, "err_done", 2 * b)
                wait(act, "copied", b)
                act.wait_ge(S["xt_done"], b + 1)
                a.activation(xnt[:], bank[0][:], ACT.Copy, accum_out=xsum[:, bass.ds(b, 1)]
                             ).then_inc(S["xnt_ready"], 1)

            def sigmoid(i, c):
                b = 2 * i + c
                wait(act, "ds_ready", b - 1)
                act.wait_ge(S["pre_done"], b + 1)
                a.activation(sg[:, c % 2], bank[1][:], ACT.Sigmoid).then_inc(S["sig_ready"], 1)
                wait(act, "ds1_ready", b)
                act.wait_ge(S["sig_ready"], b + 1)
                a.activation(one_less[:], sg[:, c % 2], ACT.Copy, bias=1.0, scale=-1.0
                             ).then_inc(S["one_less_ready"], 1)

            def turn_a1(i, c):
                b = 2 * i + c
                wait(act, "err_done", 2 * b)
                act.wait_ge(S["at_done"], b + 1)
                a.activation(a1t[:], bank[2][:], ACT.Copy).then_inc(S["a1t_ready"], 1)

            def turn_err(i, c):
                b = 2 * i + c
                wait(act, "dw_done", b)
                act.wait_ge(S["et_done"], b + 1)
                a.activation(ert[:], bank[4][:], ACT.Copy).then_inc(S["ert_ready"], 1)

            act.wait_ge(S["zeros_ready"], 1)
            a.activation(warm[:, 1:2], zeros[:, 0:1], ACT.Sigmoid)
            turn_xn(0, 0)
            sigmoid(0, 0)
            turn_a1(0, 0)
            turn_xn(0, 1)
            with act.Fori(0, NB // 2 - 1) as i:
                for c in (1, 2):
                    turn_err(i, c - 1)
                    sigmoid(i, c)
                    turn_a1(i, c)
                    turn_xn(i, c + 1)
            turn_err(0, NB - 2)
            sigmoid(0, NB - 1)
            act.wait_ge(S["gate_step"], 2)
            a.activation(gs[:], gp[:], ACT.Sigmoid).then_inc(S["gates_ready"], 1)
            turn_a1(0, NB - 1)
            for h in range(2):
                act.wait_ge(S["et_done"], NB + h)
                a.activation(ert[:, 2 * P * h:2 * P * (h + 1)], turned_half(h), ACT.Copy
                             ).then_inc(S["ert_ready"], 1)
            a.activation(warm[:, 0:1], gs[:, 0:1], ACT.Silu).then_inc(S["warmed"], 1)
            act.wait_ge(S["mz_mm"], 1)
            a.activation(n2[:], bank[5][:, 0:P], ACT.Copy).then_inc(S["n2_ready"], 1)

            def silu(i, c):
                b = 2 * i + c
                wait(act, "o_done", b)
                act.wait_ge(S["z_done"], b + 1)
                a.activation(st[:], bank[0][:], ACT.Silu).then_inc(S["silu_ready"], 1)

            def turn_x1(i, c):
                b = 2 * i + c
                wait(act, "lg_done", b)
                act.wait_ge(S["x1t_done"], b + 1)
                a.activation(x1t[:], bank[2][:], ACT.Copy).then_inc(S["x1t_ready"], 1)

            def weights_hi(e):
                act.wait_ge(S["centred"], e + 1)
                a.activation(f32r(w1_hi[:, e, :]), centre_bank(e), ACT.Copy).then_inc(S["hi_ready"], 1)

            def base_rows():
                act.wait_ge(S["nm_ready"], 6)
                for k in range(3 * BT, TILES):
                    ins = a.activation(tile(xr, k), rows[:, k, 0:D], ACT.Identity, bias=nmr2[:, k:k + 1],
                                       scale=rs2p[:, k:k + 1])
                ins.then_inc(S["base_ready"], 1)

            def keep_x1(i, c):
                b = 2 * i + c
                act.wait_ge(S["o_done"], b + 1)
                a.activation(rows[:, bass.ds(GROUP * b, GROUP), 0:D],
                             bank[1][:].rearrange("p (g d) -> p g d", d=P), ACT.Copy
                             ).then_inc(S["x1_ready"], 1)

            silu(0, 0)
            keep_x1(0, 0)
            silu(0, 1)
            turn_x1(0, 0)
            keep_x1(0, 1)
            with act.Fori(0, NB // 2 - 1) as i:
                for c in (0, 1):
                    silu(i, c + 2)
                    turn_x1(i, c + 1)
                    keep_x1(i, c + 2)
            turn_x1(0, NB - 1)

            for e in range(E):
                weights_hi(e)

            def turn_t(i, c):
                e = 2 * i + c
                wait(act, "h_mm", 2 * FC * e)
                act.wait_ge(S["tt_mm"], e + 1)
                a.activation(f32r(tt_hi[:, 0:4 * P]), bank[6][:], ACT.Copy)
                a.activation(f32r(tt_hi[:, 4 * P:]), bank[7][:, 0:P], ACT.Copy).then_inc(S["tt_hi_ready"], 1)

            def relu(i, c):
                e = 2 * i + c
                for k in range(2 * FC):
                    half, f = divmod(k, FC)
                    act.wait_ge(S["h_mm"], 2 * FC * e + k + 1)
                    if k == 0:
                        wait(act, "y_mm", ST * e)
                    a.activation(ht[:, f, half * HALF:(half + 1) * HALF], bank[k % 4][:, 0:HALF], ACT.Relu
                                 ).then_inc(S["h_ready"], 1)

            def tanh(i, c):
                e = 2 * i + c
                wait(act, "rat_ready", e)
                act.wait_ge(S["dd_ready"], e + 1)
                a.activation(th[:], dd[:], ACT.Tanh, scale=0.5).then_inc(S["th_ready"], 1)

            turn_t(0, 0)
            relu(0, 0)
            tanh(0, 0)
            turn_t(0, 1)
            base_rows()
            tanh(0, 1)
            relu(0, 1)
            turn_t(0, 2)
            with act.Fori(0, E // 2 - 2) as i:
                for c in (2, 3):
                    tanh(i, c)
                    relu(i, c)
                    turn_t(i, c + 1)
            tanh(0, E - 2)
            relu(0, E - 2)
            turn_t(0, E - 1)
            tanh(0, E - 1)
            relu(0, E - 1)

        @block.vector
        def _(dve):
            v = nc.vector

            def carry():
                v.memset(spare[:, 2:3], 0.0)

            def stats(i, c):
                b = 2 * i + c
                dve.wait_ge(x_loaded[c % 2], 16 * (i + c // 2 + 1))
                wait(dve, "mv_ready", b)
                carry()
                for k in range(GROUP):
                    ins = v.bn_stats(stat[:, k, :], xr[:, bass.ds(COLS * b + P * k, P)])
                ins.then_inc(S["mv_stat"], 1)
                wait(dve, "xn_ready", b - 1)
                dve.wait_ge(S["mv_stat"], b + 1)
                carry()
                for k in range(GROUP):
                    ins = v.bn_aggr(mv[:, c % 2, k, :], stat[:, k, :])
                ins.then_inc(S["mv_ready"], 1)

            def normalise(i, c):
                b = 2 * i + c
                wait(dve, "gt_done", b - 1)
                dve.wait_ge(S["rstd_ready"], b + 1)
                for k in range(GROUP):
                    ins = v.tensor_scalar(xn[:, c % 2, k * P:(k + 1) * P], xr[:, bass.ds(COLS * b + P * k, P)],
                                          mv[:, c % 2, k, 0:1], rs[:, c % 2, k:k + 1], ALU.subtract, ALU.mult)
                ins.then_inc(S["xn_ready"], 1)

            def make_a1(i, c):
                b = 2 * i + c
                wait(dve, "g1_done", b - 1)
                wait(dve, "ds_ready", b - 1)
                dve.wait_ge(S["sig_ready"], b + 1)
                for h in range(2):
                    cols = slice(2 * P * h, 2 * P * (h + 1))
                    v.tensor_tensor(a1[:, c % 2, cols], bank[1][:, cols], sg[:, c % 2, cols], ALU.mult
                                    ).then_inc(S["a1_ready"], 1)

            def make_d1(i, c):
                b = 2 * i + c
                dve.wait_ge(S["dw_done"], b + 1)
                wait(dve, "gt_done", b)
                dve.wait_ge(S["ds_ready"], b + 1)
                v.tensor_tensor(d1[:], bank[5][:], ds[:, c % 2], ALU.mult).then_inc(S["d1_ready"], 1)

            def clip_err(i, c):
                b = 2 * i + c
                for h in range(2):
                    dve.wait_ge(S["err_done"], 2 * b + h + 1)
                    if h == 0:
                        wait(dve, "g1_done", b)
                    v.tensor_scalar(er[:, h * 2 * P:(h + 1) * 2 * P], err_bank(h)[:, 0:2 * P], ERR_CLIP, -ERR_CLIP,
                                    ALU.min, ALU.max).then_inc(S["clip_ready"], 1)

            v.memset(zeros[:], 0.0).then_inc(S["zeros_ready"], 1)
            stats(0, 0)
            stats(0, 1)
            normalise(0, 0)
            dve.wait_ge(S["wts_loaded"], 16)
            v.tensor_scalar(nwv[:], w(WVT), -1.0, None, ALU.mult).then_inc(S["setup_ready"], 1)
            dve.wait_ge(S["setup_mm"], 1)
            v.tensor_copy(a_w[:], bank[7][:, 0:P]).then_inc(S["setup_ready"], 1)
            dve.wait_ge(S["setup_mm"], 2)
            v.tensor_copy(wr_c[:], bank[5][:, 0:E]).then_inc(S["setup_ready"], 1)
            normalise(0, 1)
            make_a1(0, 0)
            clip_err(0, 0)
            v.memset(empty[:], 0.0).then_inc(S["empty_ready"], 1)
            dve.wait_ge(S["empty_ready"], 1)
            v.memset(empty[:, :, C_ID:C_ID + 1].bitcast(I32), int(NO_TOKEN)).then_inc(S["empty_ready"], 1)
            dve.wait_ge(S["small_loaded"], 32)
            for k in range(3):
                v.tensor_copy(gate_w[:, k * P:(k + 1) * P], gw[:, k:k + 1].to_broadcast([P, P])
                              ).then_inc(S["dve_consts"], 1)
            with dve.Fori(0, NB // 2 - 1) as i:
                for c in (1, 2):
                    stats(i, c + 1)
                    make_a1(i, c)
                    make_d1(i, c - 1)
                    normalise(i, c + 1)
                    clip_err(i, c)
            dve.wait_ge(S["gates_mm"], 1)
            v.reduce_sum(gl[:], bank[7][:, 0:3 * NB].rearrange("p (g b) -> p g b", g=3), AX
                         ).then_inc(S["gate_step"], 1)
            dve.wait_ge(S["gate_step"], 1)
            v.scalar_tensor_tensor(out=gp[:], in0=gl[:], scalar=1.0 / T, in1=gate_b[:], op0=ALU.mult,
                                   op1=ALU.add).then_inc(S["gate_step"], 1)
            make_a1(0, NB - 1)
            make_d1(0, NB - 2)
            dve.wait_ge(S["gates_ready"], 1)
            v.tensor_scalar(gk[:, 0:1], gs[:, 0:1], -1.0, 1.0, ALU.mult, ALU.add)
            v.tensor_scalar(gk[:, 1:2], gs[:, 1:2], -SCALE, None, ALU.mult)
            v.tensor_scalar(gk[:, 2:3], gs[:, 2:3], 0.0, None, ALU.mult).then_inc(S["upd_step"], 1)
            dve.wait_ge(S["upd_step"], 1)
            v.tensor_scalar(base0[:], w(W0T), gk[:, 0:1], gk[:, 2:3], ALU.mult, ALU.add)
            v.tensor_scalar(base1[:], w(W1N), gk[:, 0:1], gk[:, 2:3], ALU.mult, ALU.add
                            ).then_inc(S["upd_step"], 1)
            dve.wait_ge(S["consts_ready"], 7)
            v.tensor_copy(rank[:], rank[:].bitcast(I32)).then_inc(S["dve_consts"], 1)
            v.memset(hot[:, 0, 0, :], 0.0).then_inc(S["dve_consts"], 1)
            clip_err(0, NB - 1)
            dve.wait_ge(S["ds_ready"], NB)
            dve.wait_ge(S["gt_done"], NB - 1)
            for h in range(2):
                cols = slice(2 * P * h, 2 * P * (h + 1))
                dve.wait_ge(S["dw_done"], NB + h)
                v.tensor_tensor(d1[:, cols], back_of_half(h), ds[:, (NB - 1) % 2, cols], ALU.mult
                                ).then_inc(S["d1_ready"], 1)
            LIMIT = GRAD_CLIP / SCALE
            dve.wait_ge(S["gt_done"], NB)
            v.tensor_copy(gt[:], bank[6][:, P:2 * P]).then_inc(S["gt_ready"], 1)
            v.tensor_scalar(c1[:], bank[6][:, 0:P], LIMIT, -LIMIT, ALU.min, ALU.max).then_inc(S["upd_step"], 1)
            dve.wait_ge(S["upd_step"], 3)
            v.scalar_tensor_tensor(out=w1n[:], in0=c1[:], scalar=gk[:, 1:2], in1=base1[:], op0=ALU.mult,
                                   op1=ALU.add).then_inc(S["w1_ready"], 1)
            dve.wait_ge(S["g0_mm"], 1)
            v.tensor_scalar(c0[:], bank[7][:, 0:P], LIMIT, -LIMIT, ALU.min, ALU.max).then_inc(S["upd_step"], 1)
            dve.wait_ge(S["upd_step"], 4)
            v.scalar_tensor_tensor(out=w0n[:], in0=c0[:], scalar=gk[:, 1:2], in1=base0[:], op0=ALU.mult,
                                   op1=ALU.add).then_inc(S["w0_ready"], 1)
            dve.wait_ge(S["mz_mm"], 2)
            v.tensor_copy(mz[:], bank[7][:, 0:P]).then_inc(S["mz_ready"], 1)

            def router(i, c):
                b = 2 * i + c
                lg = bank[3][:, 0:GROUP * E].rearrange("p (g e) -> p g e", e=E)
                ps = bank[4][:, 0:GROUP * E].rearrange("p (g e) -> p g e", e=E)
                d = rows[:, bass.ds(GROUP * b, GROUP), C_D:C_D + E]

                def wide(t):
                    return t[:].rearrange("p (g o) -> p g o", o=1).to_broadcast([P, GROUP, E])

                def s0():
                    dve.wait_ge(S["lg_done"], b + 1)
                    v.reduce_max(mx[:], lg, AX).then_inc(S["mx_ready"], 1)

                def s1():
                    dve.wait_ge(S["mx_ready"], b + 1)
                    v.tensor_tensor(d, lg, wide(mx), ALU.subtract).then_inc(S["d_ready"], 1)

                def s2():
                    dve.wait_ge(S["d_ready"], b + 1)
                    v.scalar_tensor_tensor(
                        out=cand[:], in0=d, scalar=0.0,
                        in1=rank[:].rearrange("p (o e) -> p o e", o=1).to_broadcast([P, GROUP, E]),
                        op0=ALU.is_ge, op1=ALU.mult).then_inc(S["cand_ready"], 1)

                def s3():
                    dve.wait_ge(S["cand_ready"], b + 1)
                    v.reduce_max(best[:], cand[:], AX).then_inc(S["best_ready"], 1)

                def s4():
                    dve.wait_ge(S["best_ready"], b + 1)
                    v.tensor_tensor(hot[:, c % 2, 1:, :], cand[:], wide(best), ALU.is_equal
                                    ).then_inc(S["hot_ready"], 1)

                def s5():
                    dve.wait_ge(S["hot_ready"], b + 1)
                    with nc.allow_low_precision("counts up to 32 are exact in bfloat16"):
                        v.reduce_sum(hot[:, 1 - c % 2, 0, :], hot[:, c % 2].rearrange("p g e -> p e g"), AX
                                     ).then_inc(S["count_ready"], 1)

                def s6():
                    dve.wait_ge(S["pos_mm"], b + 1)
                    v.tensor_tensor(own[:], ps, hot[:, c % 2, 1:, :], ALU.mult).then_inc(S["own_ready"], 1)

                def s7():
                    dve.wait_ge(S["own_ready"], b + 1)
                    v.reduce_sum(pos[:], own[:], AX).then_inc(S["pos_ready"], 1)

                def s8():
                    dve.wait_ge(S["pos_ready"], b + 1)
                    v.scalar_tensor_tensor(out=slot[:], in0=best[:], scalar=-float(CAP), in1=pos[:],
                                           op0=ALU.mult, op1=ALU.add).then_inc(S["slot_ready"], 1)
                    v.tensor_scalar(over[:], pos[:], float(CAP), NO_SLOT, ALU.is_ge, ALU.mult
                                    ).then_inc(S["over_ready"], 1)

                def s9():
                    dve.wait_ge(S["over_ready"], b + 1)
                    v.scalar_tensor_tensor(out=idx[:, bass.ds(GROUP * b, GROUP)], in0=slot[:],
                                           scalar=float(E * CAP), in1=over[:], op0=ALU.add, op1=ALU.add
                                           ).then_inc(S["idx_ready"], 1)

                return [s0, s1, s2, s3, s4, s5, s6, s7, s8, s9]

            def stats2(i, c):
                b = 2 * i + c

                def one(k):
                    def step():
                        if k == 0:
                            wait(dve, "mv2_ready", 2 * b)
                            dve.wait_ge(S["x1_ready"], b + 1)
                            carry()
                        ins = v.bn_stats(stat2[:, k, :], rows[:, bass.ds(GROUP * b + k, 1), 0:D
                                                              ].rearrange("p a d -> p (a d)"))
                        if k == GROUP - 1:
                            ins.then_inc(S["stat2_done"], 1)
                    return step

                def aggr(k):
                    def step():
                        if k == 0:
                            dve.wait_ge(S["stat2_done"], b + 1)
                            carry()
                        ins = v.bn_aggr(mv2[:, k, :], stat2[:, k, :])
                        if k == GROUP - 1:
                            ins.then_inc(S["mv2_ready"], 1)
                    return step

                def put():
                    dve.wait_ge(S["mv2_ready"], 2 * b + 1)
                    v.tensor_copy(rows[:, bass.ds(GROUP * b, GROUP), C_MEAN:C_VAR + 1], mv2[:]
                                  ).then_inc(S["mv2_ready"], 1)

                return [one(k) for k in range(GROUP)], [aggr(k) for k in range(GROUP)] + [put]

            def second(i, c, last=False):
                r = router(i, c)
                s, g = stats2(i, c + 1)
                if last:
                    order = r
                else:
                    order = r[:5] + [s[0], r[5], s[1], r[6], s[2], r[7], s[3], r[8], g[0], r[9]] + g[1:]
                for step in order:
                    step()

            dve.wait_ge(S["dve_consts"], 5)
            s, g = stats2(0, 0)
            for step in s + g:
                step()
            with dve.Fori(0, NB // 2 - 1) as i:
                second(i, 0)
                second(i, 1)
            second(0, NB - 2)
            second(0, NB - 1, last=True)

            def weights_lo(e):
                dve.wait_ge(S["hi_ready"], e + 1)
                v.tensor_tensor(f32r(w1_lo[:, e, :]), centre_bank(e), w1_hi[:, e, :], ALU.subtract
                                ).then_inc(S["lo_ready"], 1)

            for e in range(E):
                weights_lo(e)

            def base_scales(h):
                k = slice(TILES // 2 * h, TILES // 2 * (h + 1))
                dve.wait_ge(S["rs2_ready"], h + 1)
                v.tensor_scalar(rs2p[:, k], rs2[:, k], 1.0, None, ALU.add).then_inc(S["nm_ready"], 1)
                v.scalar_tensor_tensor(out=nmr2[:, k], in0=rs2[:, k], scalar=-1.0, in1=rows[:, k, C_MEAN],
                                       op0=ALU.mult, op1=ALU.mult).then_inc(S["nm_ready"], 2)
                dve.wait_ge(S["nm_ready"], 3 * (h + 1))

            def base_rows(q):
                for k in range(BT * q, BT * (q + 1)):
                    ins = v.tensor_scalar(tile(xr, k), rows[:, k, 0:D], rs2p[:, k:k + 1], nmr2[:, k:k + 1],
                                          ALU.mult, ALU.add)
                ins.then_inc(S["base_ready_v"], 1)

            def of(e, part):
                return dr[:, bass.ds(e, 1), :, part].rearrange("p e s c -> p (e s) c")

            def rest_t(i, c):
                e = 2 * i + c
                dve.wait_ge(S["tt_hi_ready"], e + 1)
                v.tensor_tensor(f32r(tt_lo[:, 0:4 * P]), bank[6][:], tt_hi[:, 0:4 * P], ALU.subtract)
                v.tensor_tensor(f32r(tt_lo[:, 4 * P:]), bank[7][:, 0:P], tt_hi[:, 4 * P:], ALU.subtract
                                ).then_inc(S["tt_lo_ready"], 1)

            def scaled(i, c):
                e = 2 * i + c
                wait(dve, "th_ready", e)
                dve.wait_ge(S["rs3_ready"], e + 1)
                v.tensor_tensor(dd[:], of(e, slice(C_D, C_D + E)),
                                rs3[:, c % 2].rearrange("p (s o) -> p s o", o=1).to_broadcast([P, ST, E]),
                                ALU.mult).then_inc(S["dd_ready"], 1)

            def pmax(i, c):
                e = 2 * i + c
                dve.wait_ge(S["th_ready"], e + 1)
                v.tensor_scalar(den[:], th[:], -1.0, 1.0, ALU.mult, ALU.add).then_inc(S["den_ready"], 1)
                dve.wait_ge(S["den_ready"], e + 1)
                v.reciprocal(rat[:], den[:]).then_inc(S["rat_ready"], 1)
                dve.wait_ge(S["rat_ready"], e + 1)
                v.scalar_tensor_tensor(out=den[:], in0=th[:], scalar=1.0, in1=rat[:], op0=ALU.add,
                                       op1=ALU.mult).then_inc(S["esum_ready"], 1)
                dve.wait_ge(S["esum_ready"], 2 * e + 1)
                v.reduce_sum(esum[:], den[:], AX).then_inc(S["esum_ready"], 1)
                dve.wait_ge(S["esum_ready"], 2 * e + 2)
                v.reciprocal(pm[:], esum[:]).then_inc(S["pm_ready"], 1)
                wait(dve, "fin_ready", ST * e)
                dve.wait_ge(S["pm_ready"], e + 1)
                v.tensor_tensor(yscale[:], pm[:], rs3[:, c % 2], ALU.mult).then_inc(S["yscale_ready"], 1)

            def finish(i, c, first):
                e = 2 * i + c
                if not first:
                    dve.wait_ge(sent[c % 2], 16 * ST * (i + c // 2))
                v.tensor_copy(ids[:, c % 2].rearrange("p (s o) -> p s o", o=1),
                              of(e, slice(C_ID, C_ID + 1)).bitcast(I32))
                dve.wait_ge(S["yscale_ready"], e + 1)
                row = of(e, slice(0, ROW))
                for s in range(ST):
                    y, last = y_tile(s)
                    if s % 2 == 0:
                        dve.wait_ge(S["y_mm"], ST * e + last + 1)
                    v.scalar_tensor_tensor(out=orow[:, c % 2, s, :], in0=y, scalar=yscale[:, s:s + 1],
                                           in1=row[:, s, 0:D], op0=ALU.mult, op1=ALU.add
                                           ).then_inc(S["fin_ready"], 1)

            def expert(i, c, first=False, last=False):
                pmax(i, c)
                if not last:
                    rest_t(i, c + 1)
                    scaled(i, c + 1)
                finish(i, c, first)

            base_scales(0)
            base_rows(0)
            rest_t(0, 0)
            base_rows(1)
            base_scales(1)
            base_rows(2)
            scaled(0, 0)
            expert(0, 0, first=True)
            expert(0, 1, first=True)
            with dve.Fori(0, E // 2 - 2) as i:
                expert(i, 2)
                expert(i, 3)
            expert(0, E - 2)
            expert(0, E - 1, last=True)

        @block.tensor
        def _(pe):
            t = nc.tensor

            def turn(dst, src, n=GROUP):
                for k in range(n):
                    ins = t.transpose(tile(dst, k), tile(src, k), ident[:])
                return ins

            def turn_xn(i, c):
                b = 2 * i + c
                wait(pe, "xnt_ready", b)
                pe.wait_ge(S["xn_ready"], b + 1)
                turn(bank[0], xn[:, c % 2]).then_inc(S["xt_done"], 1)

            def pre(i, c):
                b = 2 * i + c
                wait(pe, "a1_ready", 2 * b)
                pe.wait_ge(S["xnt_ready"], b + 1)
                for k in range(GROUP):
                    ins = t.matmul(tile(bank[1], k), tile(xnt, k), a_w[:], start=True, stop=True)
                ins.then_inc(S["pre_done"], 1)

            def turn_a1(i, c):
                b = 2 * i + c
                wait(pe, "a1t_ready", b)
                for k in range(GROUP):
                    if k % 2 == 0:
                        pe.wait_ge(S["a1_ready"], 2 * b + k // 2 + 1)
                    ins = t.transpose(tile(bank[2], k), tile(a1[:, c % 2], k), ident[:])
                ins.then_inc(S["at_done"], 1)

            def err(i, c):
                b = 2 * i + c
                wait(pe, "clip_ready", 2 * b)
                pe.wait_ge(S["a1t_ready"], b + 1)
                for k in range(GROUP):
                    o = tile(err_bank(k // 2), k % 2)
                    t.matmul(o, tile(a1t, k), w(W1T), start=True, stop=False)
                    ins = t.matmul(o, tile(xnt, k), nwv[:], start=False, stop=True)
                    if k % 2:
                        ins.then_inc(S["err_done"], 1)

            def turn_err(i, c):
                b = 2 * i + c
                wait(pe, "ert_ready", b)
                pe.wait_ge(S["clip_ready"], 2 * b + 1)
                for k in range(GROUP):
                    if k == 2:
                        pe.wait_ge(S["clip_ready"], 2 * b + 2)
                    ins = t.transpose(tile(bank[4], k), tile(er, k), ident[:])
                ins.then_inc(S["et_done"], 1)

            def back(i, c):
                b = 2 * i + c
                wait(pe, "d1_ready", b)
                pe.wait_ge(S["ert_ready"], b + 1)
                for k in range(GROUP):
                    ins = t.matmul(tile(bank[5], k), tile(ert, k), w(W1N), start=True, stop=True)
                ins.then_inc(S["dw_done"], 1)

            def grad1_tiles(i, c, tiles):
                for k in tiles:
                    ins = t.matmul(bank[6][:, 0:P], tile(er, k), tile(a1[:, c % 2], k), start=False, stop=False,
                                   skip_group_check=True)
                return ins

            def grad0_tiles(i, c, tiles):
                for k in tiles:
                    ins = t.matmul(bank[6][:, P:2 * P], tile(xn[:, c % 2], k), tile(d1, k), start=False,
                                   stop=False, skip_group_check=True)
                return ins

            def grad0(i, c):
                pe.wait_ge(S["d1_ready"], 2 * i + c + 1)
                grad0_tiles(i, c, range(GROUP)).then_inc(S["gt_done"], 1)

            def turn_err_half(h):
                pe.wait_ge(S["clip_ready"], 2 * (NB - 1) + h + 1)
                for k in (0, 1):
                    ins = t.transpose(tile(turned_half(h), k), tile(er, 2 * h + k), ident[:])
                ins.then_inc(S["et_done"], 1)

            def back_half(h):
                pe.wait_ge(S["ert_ready"], NB + h)
                for k in (0, 1):
                    ins = t.matmul(tile(back_of_half(h), k), tile(ert, 2 * h + k), w(W1N), start=True, stop=True)
                ins.then_inc(S["dw_done"], 1)

            def grad0_half(h):
                pe.wait_ge(S["d1_ready"], NB + h)
                return grad0_tiles(0, NB - 1, (2 * h, 2 * h + 1))

            def keep_clock(n, b):
                for _ in range(n):
                    t.matmul(bank[b][:, 0:2 * P], zeros[:, 0:P], zeros[:], start=True, stop=True)

            pe.wait_ge(S["zeros_ready"], 1)
            t.matmul(bank[6][:, 0:2 * P], zeros[:, 0:P], zeros[:], start=True, stop=True)
            keep_clock(5, 7)
            pe.wait_ge(S["ident_ready"], 2)
            turn_xn(0, 0)
            pe.wait_ge(S["wts_loaded"], 16)
            t.matmul(bank[7][:, 0:P], w(WK), w(W0T), start=True, stop=True).then_inc(S["setup_mm"], 1)
            pe.wait_ge(S["consts_ready"], 3)
            pe.wait_ge(S["small_loaded"], 32)
            t.matmul(bank[5][:, 0:E], centre[:], gw[:, 3:3 + E], start=True, stop=True
                     ).then_inc(S["setup_mm"], 1)
            pe.wait_ge(S["setup_ready"], 3)
            pre(0, 0)
            turn_xn(0, 1)
            turn_a1(0, 0)
            err(0, 0)
            with pe.Fori(0, NB // 2 - 1) as i:
                for c in (1, 2):
                    turn_err(i, c - 1)
                    grad1_tiles(i, c - 1, (0, 1))
                    pre(i, c)
                    back(i, c - 1)
                    grad1_tiles(i, c - 1, (2, 3)).then_inc(S["g1_done"], 1)
                    turn_a1(i, c)
                    grad0(i, c - 1)
                    err(i, c)
                    turn_xn(i, c + 1)
            turn_err(0, NB - 2)
            grad1_tiles(0, NB - 2, (0, 1))
            pre(0, NB - 1)
            pe.wait_ge(S["dve_consts"], 3)
            for k in range(3):
                ins = t.matmul(bank[7][:, k * NB:(k + 1) * NB], tile(gate_w, k), xsum[:], start=True, stop=True)
            ins.then_inc(S["gates_mm"], 1)
            back(0, NB - 2)
            grad1_tiles(0, NB - 2, (2, 3)).then_inc(S["g1_done"], 1)
            turn_a1(0, NB - 1)
            grad0(0, NB - 2)
            pe.wait_ge(S["gate_step"], 1)
            err(0, NB - 1)
            turn_err_half(0)
            grad1_tiles(0, NB - 1, (0, 1))
            turn_err_half(1)
            back_half(0)
            grad1_tiles(0, NB - 1, (2, 3)).then_inc(S["g1_done"], 1)
            back_half(1)
            grad0_half(0)
            grad0_half(1).then_inc(S["gt_done"], 1)
            keep_clock(1, 4)
            pe.wait_ge(S["gt_ready"], 1)
            t.matmul(bank[7][:, 0:P], w(WKT), gt[:], start=True, stop=True).then_inc(S["g0_mm"], 1)
            pe.wait_ge(S["w1_ready"], 1)
            t.matmul(bank[5][:, 0:P], w1n[:], w(WOT), start=True, stop=True).then_inc(S["mz_mm"], 1)
            keep_clock(1, 4)
            pe.wait_ge(S["w0_ready"], 1)
            t.matmul(bank[7][:, 0:P], w(WQ), w0n[:], start=True, stop=True).then_inc(S["mz_mm"], 1)
            keep_clock(1, 4)

            def hidden(i, c):
                b = 2 * i + c
                wait(pe, "silu_ready", b)
                t.matmul(bank[0][:], mz[:], xnt_all[:, bass.ds(COLS * b, COLS)], start=True, stop=True
                         ).then_inc(S["z_done"], 1)

            def output(i, c):
                b = 2 * i + c
                pe.wait_ge(S["silu_ready"], b + 1)
                for k in range(GROUP):
                    ins = t.matmul(tile(bank[1], k), tile(st, k), n2[:], start=False, stop=True,
                                   skip_group_check=True)
                ins.then_inc(S["o_done"], 1)

            def residual(i, c):
                b = 2 * i + c
                wait(pe, "x1_ready", b)
                t.matmul(bank[1][:], ident[:], xr[:, bass.ds(COLS * b, COLS)], start=True, stop=False,
                         skip_group_check=True)

            def turn_x1(i, c):
                b = 2 * i + c
                wait(pe, "x1t_ready", b)
                pe.wait_ge(S["x1_ready"], b + 1)
                for k in range(GROUP):
                    ins = t.transpose(tile(bank[2], k), x1_tile(i, c, k), ident[:])
                ins.then_inc(S["x1t_done"], 1)

            def x1_tile(i, c, k):
                return rows[:, GROUP * (2 * i + c) + k, 0:D]

            def logits(i, c):
                b = 2 * i + c
                wait(pe, "d_ready", b)
                pe.wait_ge(S["x1t_ready"], b + 1)
                for k in range(GROUP):
                    ins = t.matmul(bank[3][:, k * E:(k + 1) * E], tile(x1t, k), wr_c[:], start=True, stop=True)
                ins.then_inc(S["lg_done"], 1)

            def positions(i, c):
                b = 2 * i + c
                wait(pe, "count_ready", b)
                wait(pe, "own_ready", b)
                pe.wait_ge(S["hot_ready"], b + 1)
                ps = bank[4][:, 0:GROUP * E]
                h = hot[:, c % 2]
                t.matmul(ps, upper[:], h[:, 1:, :].rearrange("p g e -> p (g e)"), start=True, stop=False)
                for k in range(GROUP):
                    n = GROUP - k
                    ins = t.matmul(ps[:, k * E:].rearrange("p (g e) -> p g e", e=E), ones[:],
                                   h[:, k:k + 1, :].to_broadcast([P, n, E]), start=False,
                                   stop=(k == GROUP - 1))
                ins.then_inc(S["pos_mm"], 1)

            pe.wait_ge(S["mz_ready"], 1)
            hidden(0, 0)
            residual(0, 0)
            pe.wait_ge(S["n2_ready"], 1)
            output(0, 0)
            hidden(0, 1)
            pe.wait_ge(S["consts_ready"], 6)
            turn_x1(0, 0)
            residual(0, 1)
            logits(0, 0)
            output(0, 1)
            for b in range(NB - 2):
                hidden(0, b + 2)
                positions(0, b)
                turn_x1(0, b + 1)
                residual(0, b + 2)
                logits(0, b + 1)
                output(0, b + 2)

            def centre_w(e):
                wait(pe, "lo_ready", e - 3)
                t.matmul(centre_bank(e), centre[:], w1_in[:, F * e:F * (e + 1)], start=True, stop=True
                         ).then_inc(S["centred"], 1)

            positions(0, NB - 2)
            turn_x1(0, NB - 1)
            pe.wait_ge(S["w_up_loaded"], 16)
            pe.wait_ge(S["silu_ready"], NB)
            centre_w(0)
            logits(0, NB - 1)
            centre_w(1)
            positions(0, NB - 1)
            for e in range(2, E):
                centre_w(e)

            def turn_t(e):
                pe.wait_ge(dr_loaded[e % 2], 16 * (e // 2 + 1))
                wait(pe, "tt_lo_ready", e)
                for s in range(ST):
                    o = tile(bank[6], s) if s < 4 else bank[7][:, 0:P]
                    ins = t.transpose(o, dr[:, e, s, 0:D], ident[:])
                ins.then_inc(S["tt_mm"], 1)

            def layer1(e):
                pe.wait_ge(S["tt_lo_ready"], e + 1)
                for k in range(2 * FC):
                    half, f = divmod(k, FC)
                    if k == 3:
                        wait(pe, "fin_ready", ST * e)
                    if k >= 4:
                        pe.wait_ge(S["h_ready"], 2 * FC * e + k - 3)
                    cols, o = slice(half * HALF, (half + 1) * HALF), bank[k % 4][:, 0:HALF]
                    hi, lo = f32r(tile(w1_hi[:, e], f)), f32r(tile(w1_lo[:, e], f))
                    t.matmul(o, hi, f32r(tt_hi[:, cols]), start=True, stop=False)
                    t.matmul(o, lo, f32r(tt_hi[:, cols]), start=False, stop=False)
                    t.matmul(o, hi, f32r(tt_lo[:, cols]), start=False, stop=True).then_inc(S["h_mm"], 1)

            def layer2(e):
                for s in range(ST):
                    if s == 0:
                        pe.wait_ge(S["h_ready"], 2 * FC * e + FC)
                    if (s + 1) * P > HALF >= s * P:
                        pe.wait_ge(S["h_ready"], 2 * FC * (e + 1))
                    y, last = y_tile(s)
                    if s % 2 == 0:
                        wait(pe, "fin_ready", ST * (e - 1) + last + 1)
                    for f in range(FC):
                        ins = t.matmul(y, ht[:, f, s * P:(s + 1) * P], w2[:, e, f, :],
                                       start=(f == 0), stop=(f == FC - 1))
                    if s == last:
                        ins.then_inc(S["y_mm"], s % 2 + 1)

            pe.wait_ge(S["lo_ready"], E)
            keep_clock(6, 4)
            turn_t(0)
            pe.wait_ge(S["w_down_loaded"], 16)
            for e in range(E):
                layer1(e)
                if e + 1 < E:
                    turn_t(e + 1)
                layer2(e)


def kernel(**inputs):
    import concourse.bacc as bacc
    from concourse.bass_utils import run_bass_kernel_spmd

    a = {k.removeprefix("L0_"): np.asarray(v) for k, v in inputs.items()}
    x = a["attn_x"]
    Wk, Wv, Wq, Wout, W0, W1 = (a["attn_" + n] for n in ("Wk", "Wv", "Wq", "Wout", "W0", "W1"))
    arrays = {
        "x": np.ascontiguousarray(x.reshape(-1, x.shape[-1])),
        "wpack": np.ascontiguousarray(np.concatenate([Wk, Wk.T, Wv.T, Wq, W0.T, W1, W1.T, Wout.T], axis=1)),
        "wsmall": np.ascontiguousarray(np.concatenate(
            [a["attn_Wg_decay"].T, a["attn_Wg_lr"].T, a["attn_Wg_mom"].T, a["ffn_Wr"]], axis=1)),
        "biases": np.concatenate([a["attn_bg_decay"], a["attn_bg_lr"], a["attn_bg_mom"]])[None, :],
        "w_up": np.ascontiguousarray(a["ffn_W1"]),
        "w_down": np.ascontiguousarray(a["ffn_W2"]),
    }
    nc = bacc.Bacc("TRN2", target_bir_lowering=False, num_devices=1)
    args = [nc.dram_tensor(f"in_{n}", v.shape, mybir.dt.from_np(v.dtype), kind="ExternalInput").ap()
            for n, v in arrays.items()]
    y = nc.dram_tensor("out_y", arrays["x"].shape, F32, kind="ExternalOutput").ap()
    build(nc, *args, y)
    r = run_bass_kernel_spmd(nc, [{f"in_{n}": v for n, v in arrays.items()}], core_ids=[0])
    return r.results[0]["out_y"].reshape(x.shape)
```

```python
from contextlib import ExitStack

import numpy as np

import concourse.bass as bass
from concourse import mybir

ALU = mybir.AluOpType
ACT = mybir.ActivationFunctionType
F32 = mybir.dt.float32
BF16 = mybir.dt.bfloat16
F32R = mybir.dt.float32r
I32 = mybir.dt.int32
U32 = mybir.dt.uint32
AX = mybir.AxisListType.X

P = 128
EPS = 1e-5
ERR_CLIP = 5.0
GRAD_CLIP = 1.0
SCALE = 2.0 / 512.0
CAP_FACTOR = 1.25
GROUP = 4
WK, WKT, WVT, WQ, W0T, W1N, W1T, WOT = range(8)


def build(nc: bass.Bass, x: bass.AP, wpack: bass.AP, wsmall: bass.AP, biases: bass.AP,
          w_up: bass.AP, w_down: bass.AP, out: bass.AP):
    T, D = x.shape
    E, _, F = w_up.shape
    assert D == P
    TILES = T // P
    NB = TILES // GROUP
    COLS = GROUP * P
    CAP = int(CAP_FACTOR * T / E)
    ST = CAP // P
    HALF = CAP // 2
    FC = F // P
    BT = TILES // 4
    assert NB == 8 and E == 8 and CAP == ST * P and HALF <= 512 and FC == 4
    C_MEAN, C_VAR, C_D, C_ID = D, D + 1, D + 2, D + 2 + E
    ROW = C_ID + 1
    NO_SLOT = float(2 ** 20)
    NO_TOKEN = float(T)

    disp = nc.dram_tensor("disp", [E * CAP, ROW], F32, kind="Internal").ap()

    with ExitStack() as ctx:
        def sb(name, shape, dt=F32):
            return ctx.enter_context(nc.sbuf_tensor(name, shape, dt))

        def sem(name):
            return ctx.enter_context(nc.semaphore(name))

        bank = [ctx.enter_context(nc.psum_tensor(f"bank{i}", [P, 512], F32)) for i in range(8)]

        ident = sb("ident", [P, P])
        centre = sb("centre", [P, P])
        upper = sb("upper", [P, P], BF16)
        ones = sb("ones", [P, P], BF16)
        zeros = sb("zeros", [P, 2 * P])
        neg_half = sb("neg_half", [P, TILES // 2])
        eps = sb("eps", [P, TILES // 2])
        rank = sb("rank", [P, E])
        wts = sb("wts", [P, 8 * P])
        gw = sb("gw", [P, 3 + E])
        gate_w = sb("gate_w", [P, 3 * P])
        gate_b = sb("gate_b", [P, 3])
        av_hi = sb("av_hi", [P, 2 * P])
        av_lo = sb("av_lo", [P, 2 * P])
        wr_c = sb("wr_c", [P, E])
        xr = sb("xr", [P, TILES * P])
        stat = sb("stat", [P, GROUP, 6])
        mv = sb("mv", [P, 2, GROUP, 2])
        veps = sb("veps", [P, TILES // 2])
        rs = sb("rs", [P, 2, GROUP])
        xn = sb("xn", [P, 2, COLS])
        xt_hi = sb("xt_hi", [P, COLS])
        xt_lo = sb("xt_lo", [P, COLS])
        xnt_all = sb("xnt_all", [P, T])
        xsum = sb("xsum", [P, NB])
        sg = sb("sg", [P, 2, COLS])
        a1 = sb("a1", [P, 2, COLS])
        one_less = sb("one_less", [P, COLS])
        ds1 = sb("ds1", [P, COLS])
        ds = sb("ds", [P, 2, COLS])
        a1t = sb("a1t", [P, COLS])
        er = sb("er", [P, COLS])
        ert = sb("ert", [P, COLS])
        d1 = sb("d1", [P, COLS])
        gl = sb("gl", [P, 3])
        gp = sb("gp", [P, 3])
        gs = sb("gs", [P, 3])
        gk = sb("gk", [P, 3])
        base0 = sb("base0", [P, P])
        base1 = sb("base1", [P, P])
        gt = sb("gt", [P, P])
        c0 = sb("c0", [P, P])
        c1 = sb("c1", [P, P])
        w0n = sb("w0n", [P, P])
        w1n = sb("w1n", [P, P])
        mz = sb("mz", [P, P])
        n2 = sb("n2", [P, P])
        st = sg[:, 0]
        rows = sb("rows", [P, TILES, ROW])
        stat2 = sb("stat2", [P, GROUP, 6])
        mv2 = sb("mv2", [P, GROUP, 2])
        x1t = sg[:, 1]
        mx = sb("mx", [P, GROUP])
        cand = sb("cand", [P, GROUP, E])
        best = sb("best", [P, GROUP])
        hot = sb("hot", [P, 2, GROUP + 1, E], BF16)
        own = sb("own", [P, GROUP, E])
        pos = sb("pos", [P, GROUP])
        slot = sb("slot", [P, GROUP])
        over = sb("over", [P, GROUP])
        idx = sb("idx", [P, TILES], I32)
        rs2 = sb("rs2", [P, TILES])
        rs2p = sb("rs2p", [P, TILES])
        nmr2 = sb("nmr2", [P, TILES])
        empty = sb("empty", [P, ST, ROW])
        dr = sb("dr", [P, E, ST, ROW])
        w1_in = dr[:].rearrange("p e s c -> p (e s c)")[:, 0:E * F]
        ids = sb("ids", [P, 2, ST], I32)
        ve3 = sb("ve3", [P, ST])
        rs3 = sb("rs3", [P, 2, ST])
        tt_hi = sb("tt_hi", [P, CAP])
        tt_lo = sb("tt_lo", [P, CAP])
        dd = sb("dd", [P, ST, E])
        th = sb("th", [P, ST, E])
        den = sb("den", [P, ST, E])
        rat = sb("rat", [P, ST, E])
        esum = sb("esum", [P, ST])
        pm = sb("pm", [P, ST])
        yscale = sb("yscale", [P, ST])
        w1_hi = sb("w1_hi", [P, E, F])
        w1_lo = sb("w1_lo", [P, E, F])
        w2 = sb("w2", [P, E, FC, P])
        ht = sb("ht", [P, FC, CAP])
        orow = sb("orow", [P, 2, ST, P])
        warm = sb("warm", [P, 2])
        spare = sb("spare", [P, 4])
        started = sb("started", [P, 6])

        def w(k):
            return wts[:, k * P:(k + 1) * P]

        def halves(t):
            v = t.rearrange("p (h g d) -> p h g d", h=2, d=P)
            return [v[:, h] for h in range(2)]

        def pair(k):
            return bank[(3, 7)[k // 2]][:, k % 2 * 2 * P:(k % 2 + 1) * 2 * P]

        def pre_half(h):
            return bank[(3, 7)[h]][:].rearrange("p (g t d) -> p g t d", t=2, d=P)[:, :, 0, :]

        def err_half(h):
            return bank[(3, 7)[h]][:].rearrange("p (g t d) -> p g t d", t=2, d=P)[:, :, 1, :]

        def turned_half(h):
            return bank[(4, 2)[h]][:, 0:2 * P]

        def back_of_half(h):
            return bank[(5, 1)[h]][:, 0:2 * P]

        parts = (range(0, HALF // P + 1), range(HALF // P + 1, ST))

        def part_cols(n):
            return slice(parts[n].start * P, parts[n].stop * P)

        def turned_part(n):
            return bank[6 + n][:, 0:len(parts[n]) * P]

        def centre_bank(e):
            return bank[(0, 5, 6, 7)[e % 4]][:]

        def y_tile(s, ending=False):
            groups = ((0,), (1,), (2,), (3,), (4,)) if ending else ((0, 1), (2, 3), (4,))
            banks = (4, 5, 6, 7, 4) if ending else (4, 5, 3)
            for n, tiles in zip(banks, groups):
                if s in tiles:
                    return tile(bank[n], s - tiles[0]), tiles[0], tiles[-1]

        def f32r(ap):
            return ap.bitcast(F32R)

        def tile(t, g):
            return t[:, g * P:(g + 1) * P]

        names = """wts_loaded small_loaded ident_ready consts_ready zeros_ready dve_consts empty_ready disp_init
            mv_stat mv_ready veps_ready rstd_ready xn_ready xt_done xt_hi_ready xt_lo_ready xnt_ready pre_done sig_ready one_less_ready a1_ready
            at_done a1t_ready err_done clip_ready et_done ert_ready dw_done ds1_ready ds_ready d1_ready g1_done
            gt_done setup_mm setup_ready gates_mm gate_step gates_ready upd_step gt_ready g0_mm w0_ready w1_ready
            mz_mm mz_ready n2_ready z_done silu_ready o_done x1_ready x1t_done x1t_ready lg_done
            mx_ready d_ready cand_ready best_ready hot_ready count_ready pos_mm own_ready pos_ready slot_ready
            over_ready idx_ready stat2_done mv2_ready scattered ve2_ready rs2_ready nm_ready base_ready base_ready_v
            rows_ids first_rows ve3_ready rs3_ready w_up_loaded w_down_loaded centred hi_ready lo_ready tt_mm tt_hi_ready
            tt_lo_ready h_mm h_ready y_mm base_stored yscale_ready
            dd_ready th_ready den_ready rat_ready esum_ready pm_ready fin_ready warmed""".split()
        S = {n: sem(n) for n in names}
        x_loaded = [sem(f"x_loaded{i}") for i in range(2)]
        dr_loaded = [sem(f"dr_loaded{i}") for i in range(2)]
        sent = [sem(f"sent{i}") for i in range(2)]

        from_one = ("d1_ready", "dw_done", "ds_ready", "g1_done", "gt_done", "ert_ready")

        def wait(eng, s, count):
            if isinstance(count, int) and count <= 0:
                return
            eng.wait_ge(S[s], count + 1 if s in from_one else count)

        block = ctx.enter_context(nc.Block())

        @block.sync
        def _(sp):
            def load_x(i, c):
                if isinstance(i, int) and c < 2:
                    pass
                else:
                    sp.wait_ge(x_loaded[c % 2], 16 * (i + c // 2))
                b = 2 * i + c
                sp.dma_start(xr[:, bass.ds(COLS * b, COLS)].rearrange("p (g d) -> p g d", d=P),
                             x_view[:, bass.ds(GROUP * b, GROUP), :]).then_inc(x_loaded[c % 2], 16)

            x_view = x.rearrange("(n p) d -> p n d", p=P)
            out_view = out.rearrange("(n p) d -> p n d", p=P)
            load_x(0, 0)
            load_x(0, 1)
            sp.dma_start(wts[:], wpack).then_inc(S["wts_loaded"], 16)
            sp.dma_start(gw[:], wsmall).then_inc(S["small_loaded"], 16)
            sp.dma_start(gate_b[:], biases.to_broadcast([P, 3])).then_inc(S["small_loaded"], 16)
            with sp.Fori(0, NB // 2 - 1) as i:
                load_x(i, 2)
                load_x(i, 3)
            sp.dma_start(w1_in.rearrange("p (e f) -> p e f", f=F), w_up.rearrange("e d f -> d e f")).then_inc(S["w_up_loaded"], 16)
            sp.dma_start(w2[:], w_down.rearrange("e (c p) d -> p e c d", p=P)).then_inc(S["w_down_loaded"], 16)
            sp.wait_ge(S["empty_ready"], 2)
            with sp.Fori(0, E) as e:
                sp.dma_start(disp[bass.ds(CAP * e, CAP), :].rearrange("(p s) c -> p s c", s=ST),
                             empty[:]).then_inc(S["disp_init"], 16)

            def load_rows(i, c):
                if not (isinstance(i, int) and c < 2):
                    sp.wait_ge(dr_loaded[c % 2], 16 * (i + c // 2))
                e = 2 * i + c
                sp.dma_start(dr[:, bass.ds(e, 1)].rearrange("p e s c -> p (e s c)"),
                             disp[bass.ds(CAP * e, CAP), :].rearrange("(p s) c -> p (s c)", s=ST)
                             ).then_inc(dr_loaded[c % 2], 16)

            def load_part(n, s):
                k0, k1 = parts[n].start, parts[n].stop
                sp.dma_start(dr[:, 0, k0:k1, :],
                             disp[0:CAP, :].rearrange("(p s) c -> p s c", s=ST)[:, k0:k1, :]).then_inc(s, 16)

            def store_base(q, made, count):
                k0 = BT * q
                sp.wait_ge(S[made], count)
                sp.dma_start(out_view[:, k0:k0 + BT, :],
                             xr[:, k0 * P:(k0 + BT) * P].rearrange("p (g d) -> p g d", d=P)
                             ).then_inc(S["base_stored"], 16)

            sp.wait_ge(S["centred"], E)
            sp.wait_ge(S["scattered"], 16 * TILES)
            load_part(0, S["first_rows"])
            load_part(1, dr_loaded[0])
            load_rows(0, 1)
            load_rows(0, 2)
            store_base(0, "base_ready_v", 1)
            load_rows(0, 3)
            store_base(1, "base_ready_v", 2)
            store_base(2, "base_ready_v", 3)
            store_base(3, "base_ready", 1)
            with sp.Fori(1, E // 2 - 1) as i:
                load_rows(i, 2)
                load_rows(i, 3)
            sp.wait_ge(S["base_stored"], 16 * 4)
            sp.wait_ge(sent[0], 16 * ST * E // 2)
            sp.wait_ge(sent[1], 16 * ST * E // 2)

        @block.gpsimd
        def _(pool):
            g = nc.gpsimd

            def carry(k):
                g.tensor_tensor(spare[:, k:k + 1], eps[:, 0:1], eps[:, 0:1], ALU.add)

            g.memset(ident[:], 0.0).then_inc(S["ident_ready"], 1)
            pool.wait_ge(S["ident_ready"], 1)
            g.affine_select(out=ident[:], in_=ident[:], compare_op=ALU.not_equal, fill=1.0, base=0,
                            pattern=[[-1, P]], channel_multiplier=1).then_inc(S["ident_ready"], 1)
            g.memset(eps[:], EPS)
            g.memset(neg_half[:], -0.5).then_inc(S["consts_ready"], 1)

            def rstd(i, c):
                b = 2 * i + c
                wait(pool, "rstd_ready", b)
                pool.wait_ge(S["mv_ready"], b + 1)
                g.tensor_tensor(veps[:, 0:GROUP], mv[:, c % 2, :, 1], eps[:, 0:GROUP], ALU.add
                                ).then_inc(S["veps_ready"], 1)
                wait(pool, "xn_ready", b - 1)
                pool.wait_ge(S["veps_ready"], b + 1)
                g.tensor_tensor(rs[:, c % 2, :], veps[:, 0:GROUP], neg_half[:, 0:GROUP], ALU.pow
                                ).then_inc(S["rstd_ready"], 1)

            def silu_slope(i, c):
                b = 2 * i + c
                pool.wait_ge(S["a1_ready"], 2 * b + 2)
                wait(pool, "ds_ready", b)
                pool.wait_ge(S["one_less_ready"], b + 1)
                g.tensor_tensor(ds1[:], a1[:, c % 2], one_less[:], ALU.mult).then_inc(S["ds1_ready"], 1)
                wait(pool, "d1_ready", 2 * (b - 1))
                pool.wait_ge(S["ds1_ready"], b + 1)
                g.tensor_tensor(ds[:, c % 2], sg[:, c % 2], ds1[:], ALU.add).then_inc(S["ds_ready"], 1)

            g.memset(centre[:], -1.0 / D).then_inc(S["consts_ready"], 1)
            pool.wait_ge(S["consts_ready"], 2)
            g.affine_select(out=centre[:], in_=centre[:], compare_op=ALU.not_equal, fill=1.0 - 1.0 / D, base=0,
                            pattern=[[-1, P]], channel_multiplier=1).then_inc(S["consts_ready"], 1)
            rstd(0, 0)
            rstd(0, 1)
            silu_slope(0, 0)
            g.memset(upper[:], 1.0).then_inc(S["consts_ready"], 1)
            g.memset(ones[:], 1.0).then_inc(S["consts_ready"], 1)
            pool.wait_ge(S["consts_ready"], 5)
            g.affine_select(out=upper[:], in_=upper[:], compare_op=ALU.is_gt, fill=0.0, base=0,
                            pattern=[[1, P]], channel_multiplier=-1).then_inc(S["consts_ready"], 1)
            g.iota(rank[:].bitcast(I32), pattern=[[-1, E]], base=E, channel_multiplier=0
                   ).then_inc(S["consts_ready"], 1)
            g.iota(rows[:, :, C_ID:C_ID + 1].bitcast(I32), pattern=[[P, TILES], [0, 1]], base=0,
                   channel_multiplier=1).then_inc(S["rows_ids"], 1)
            with pool.Fori(0, NB // 2 - 1) as i:
                for c in (1, 2):
                    rstd(i, c + 1)
                    silu_slope(i, c)
            silu_slope(0, NB - 1)

            pool.wait_ge(S["rows_ids"], 1)
            pool.wait_ge(S["disp_init"], 16 * E)
            for b in range(NB):
                pool.wait_ge(S["idx_ready"], b + 1)
                pool.wait_ge(S["mv2_ready"], 2 * (b + 1))
                for k in range(GROUP * b, GROUP * (b + 1)):
                    g.indirect_dma_start(
                        disp, bass.IndirectOffsetOnAxis(ap=idx[:, k:k + 1].bitcast(U32), axis=0),
                        rows[:, k, :], None, bounds_check=E * CAP - 1, oob_is_err=False
                    ).then_inc(S["scattered"], 16)

            def base_scales(h):
                n = TILES // 2
                k = slice(n * h, n * (h + 1))
                wait(pool, "rs2_ready", h)
                g.tensor_tensor(veps[:], rows[:, k, C_VAR], eps[:], ALU.add).then_inc(S["ve2_ready"], 1)
                pool.wait_ge(S["ve2_ready"], h + 1)
                g.tensor_tensor(rs2[:, k], veps[:], neg_half[:], ALU.pow).then_inc(S["rs2_ready"], 1)

            def rstd_rows(i, c):
                e = 2 * i + c
                if isinstance(i, int) and e == 0:
                    pool.wait_ge(S["first_rows"], 16)
                pool.wait_ge(dr_loaded[c % 2], 16 * (i + c // 2 + 1))
                wait(pool, "rs3_ready", e)
                g.tensor_tensor(ve3[:], dr[:, bass.ds(e, 1), :, C_VAR].rearrange("p e s -> p (e s)"), eps[:, 0:ST], ALU.add).then_inc(S["ve3_ready"], 1)
                wait(pool, "yscale_ready", e - 1)
                pool.wait_ge(S["ve3_ready"], e + 1)
                g.tensor_tensor(rs3[:, c % 2, :], ve3[:], neg_half[:, 0:ST], ALU.pow).then_inc(S["rs3_ready"], 1)

            def send_tile(c, s):
                g.indirect_dma_start(
                    out, bass.IndirectOffsetOnAxis(ap=ids[:, c % 2, s:s + 1].bitcast(U32), axis=0),
                    orow[:, c % 2, s, :], None, bounds_check=T - 1, oob_is_err=False
                ).then_inc(sent[c % 2], 16)

            def send(i, c):
                pool.wait_ge(S["fin_ready"], ST * (2 * i + c + 1))
                carry(c % 2 if c < 2 else 3)
                for s in range(ST):
                    send_tile(c, s)

            base_scales(0)
            base_scales(1)
            rstd_rows(0, 0)
            rstd_rows(0, 1)
            rstd_rows(0, 2)
            pool.wait_ge(S["base_stored"], 16 * 4)
            send(0, 0)
            rstd_rows(0, 3)
            send(0, 1)
            with pool.Fori(1, E // 2 - 1) as i:
                for c in (0, 1):
                    rstd_rows(i, c + 2)
                    send(i, c)
            for e in (E - 2, E - 1):
                for s in range(ST):
                    pool.wait_ge(S["fin_ready"], ST * e + s + 1)
                    send_tile(e, s)

        @block.scalar
        def _(act):
            a = nc.scalar

            def turn_xn(i, c):
                b = 2 * i + c
                wait(act, "pre_done", 2 * b)
                act.wait_ge(S["xt_done"], b + 1)
                a.activation(f32r(xt_hi[:]), bank[0][:], ACT.Copy).then_inc(S["xt_hi_ready"], 1)

            def keep_xn(i, c):
                b = 2 * i + c
                act.wait_ge(S["xt_lo_ready"], b + 1)
                a.activation(xnt_all[:, bass.ds(COLS * b, COLS)], bank[0][:], ACT.Copy,
                             accum_out=xsum[:, bass.ds(b, 1)]).then_inc(S["xnt_ready"], 1)

            def sigmoid(i, c):
                b = 2 * i + c
                wait(act, "ds_ready", b - 1)
                for h in range(2):
                    act.wait_ge(S["pre_done"], 2 * b + h + 1)
                    a.activation(halves(sg[:, c % 2])[h], pre_half(h), ACT.Sigmoid).then_inc(S["sig_ready"], 1)
                wait(act, "ds1_ready", b)
                act.wait_ge(S["sig_ready"], 2 * b + 2)
                a.activation(one_less[:], sg[:, c % 2], ACT.Copy, bias=1.0, scale=-1.0
                             ).then_inc(S["one_less_ready"], 1)

            def turn_a1(i, c):
                b = 2 * i + c
                wait(act, "err_done", 2 * b)
                act.wait_ge(S["at_done"], b + 1)
                a.activation(a1t[:], bank[2][:], ACT.Copy).then_inc(S["a1t_ready"], 1)

            def turn_err(i, c):
                b = 2 * i + c
                wait(act, "dw_done", b)
                act.wait_ge(S["et_done"], b + 1)
                a.activation(ert[:], bank[4][:], ACT.Copy).then_inc(S["ert_ready"], 1)

            act.wait_ge(S["zeros_ready"], 1)
            a.activation(warm[:, 1:2], zeros[:, 0:1], ACT.Sigmoid)
            turn_xn(0, 0)
            keep_xn(0, 0)
            sigmoid(0, 0)
            turn_a1(0, 0)
            turn_xn(0, 1)
            with act.Fori(0, NB // 2 - 1) as i:
                for c in (1, 2):
                    turn_err(i, c - 1)
                    keep_xn(i, c)
                    sigmoid(i, c)
                    turn_a1(i, c)
                    turn_xn(i, c + 1)
            turn_err(0, NB - 2)
            keep_xn(0, NB - 1)
            sigmoid(0, NB - 1)
            act.wait_ge(S["gate_step"], 2)
            a.activation(gs[:], gp[:], ACT.Sigmoid).then_inc(S["gates_ready"], 1)
            turn_a1(0, NB - 1)
            for h in range(2):
                act.wait_ge(S["et_done"], NB + h)
                a.activation(ert[:, 2 * P * h:2 * P * (h + 1)], turned_half(h), ACT.Copy
                             ).then_inc(S["ert_ready"], 1)
            a.activation(warm[:, 0:1], gs[:, 0:1], ACT.Silu).then_inc(S["warmed"], 1)
            act.wait_ge(S["mz_mm"], 1)
            a.activation(n2[:], bank[5][:, 0:P], ACT.Copy).then_inc(S["n2_ready"], 1)

            def silu(i, c):
                b = 2 * i + c
                wait(act, "o_done", b)
                act.wait_ge(S["z_done"], b + 1)
                a.activation(st[:], bank[0][:], ACT.Silu).then_inc(S["silu_ready"], 1)

            def turn_x1(i, c):
                b = 2 * i + c
                wait(act, "lg_done", b)
                act.wait_ge(S["x1t_done"], b + 1)
                a.activation(x1t[:], bank[2][:], ACT.Copy).then_inc(S["x1t_ready"], 1)

            def weights_hi(e):
                act.wait_ge(S["centred"], e + 1)
                a.activation(f32r(w1_hi[:, e, :]), centre_bank(e), ACT.Copy).then_inc(S["hi_ready"], 1)

            def base_rows():
                act.wait_ge(S["nm_ready"], 6)
                for k in range(3 * BT, TILES):
                    ins = a.activation(tile(xr, k), rows[:, k, 0:D], ACT.Identity, bias=nmr2[:, k:k + 1],
                                       scale=rs2p[:, k:k + 1])
                ins.then_inc(S["base_ready"], 1)

            def keep_x1(i, c):
                b = 2 * i + c
                act.wait_ge(S["o_done"], b + 1)
                a.activation(rows[:, bass.ds(GROUP * b, GROUP), 0:D],
                             bank[1][:].rearrange("p (g d) -> p g d", d=P), ACT.Copy
                             ).then_inc(S["x1_ready"], 1)

            wait(act, "ds_ready", NB)
            silu(0, 0)
            keep_x1(0, 0)
            silu(0, 1)
            turn_x1(0, 0)
            keep_x1(0, 1)
            with act.Fori(0, NB // 2 - 1) as i:
                for c in (0, 1):
                    silu(i, c + 2)
                    turn_x1(i, c + 1)
                    keep_x1(i, c + 2)
            turn_x1(0, NB - 1)

            for e in range(E):
                weights_hi(e)

            def turn_t(i, c):
                e = 2 * i + c
                wait(act, "h_mm", 2 * FC * e)
                for n in range(2):
                    act.wait_ge(S["tt_mm"], 2 * e + n + 1)
                    a.activation(f32r(tt_hi[:, part_cols(n)]), turned_part(n), ACT.Copy
                                 ).then_inc(S["tt_hi_ready"], 1)

            def relu(i, c):
                e = 2 * i + c
                for k in range(2 * FC):
                    half, f = divmod(k, FC)
                    act.wait_ge(S["h_mm"], 2 * FC * e + k + 1)
                    if k == 0:
                        wait(act, "y_mm", ST * e)
                    a.activation(ht[:, f, half * HALF:(half + 1) * HALF], bank[k % 4][:, 0:HALF], ACT.Relu
                                 ).then_inc(S["h_ready"], 1)

            def tanh(i, c):
                e = 2 * i + c
                wait(act, "rat_ready", e)
                act.wait_ge(S["dd_ready"], e + 1)
                a.activation(th[:], dd[:], ACT.Tanh, scale=0.5).then_inc(S["th_ready"], 1)

            turn_t(0, 0)
            relu(0, 0)
            tanh(0, 0)
            turn_t(0, 1)
            base_rows()
            tanh(0, 1)
            relu(0, 1)
            turn_t(0, 2)
            with act.Fori(0, E // 2 - 2) as i:
                for c in (2, 3):
                    tanh(i, c)
                    relu(i, c)
                    turn_t(i, c + 1)
            tanh(0, E - 2)
            relu(0, E - 2)
            turn_t(0, E - 1)
            tanh(0, E - 1)
            relu(0, E - 1)

        @block.vector
        def _(dve):
            v = nc.vector

            def carry():
                v.memset(spare[:, 2:3], 0.0)

            def stats(i, c):
                b = 2 * i + c
                dve.wait_ge(x_loaded[c % 2], 16 * (i + c // 2 + 1))
                wait(dve, "mv_ready", b)
                carry()
                for k in range(GROUP):
                    ins = v.bn_stats(stat[:, k, :], xr[:, bass.ds(COLS * b + P * k, P)])
                ins.then_inc(S["mv_stat"], 1)
                wait(dve, "xn_ready", b - 1)
                dve.wait_ge(S["mv_stat"], b + 1)
                carry()
                for k in range(GROUP):
                    ins = v.bn_aggr(mv[:, c % 2, k, :], stat[:, k, :])
                ins.then_inc(S["mv_ready"], 1)

            def normalise(i, c):
                b = 2 * i + c
                wait(dve, "gt_done", b - 1)
                dve.wait_ge(S["rstd_ready"], b + 1)
                for k in range(GROUP):
                    ins = v.tensor_scalar(xn[:, c % 2, k * P:(k + 1) * P], xr[:, bass.ds(COLS * b + P * k, P)],
                                          mv[:, c % 2, k, 0:1], rs[:, c % 2, k:k + 1], ALU.subtract, ALU.mult)
                ins.then_inc(S["xn_ready"], 1)

            def make_a1(i, c):
                b = 2 * i + c
                wait(dve, "g1_done", b - 1)
                wait(dve, "ds_ready", b - 1)
                for h in range(2):
                    dve.wait_ge(S["sig_ready"], 2 * b + h + 1)
                    v.tensor_tensor(halves(a1[:, c % 2])[h], pre_half(h), halves(sg[:, c % 2])[h], ALU.mult
                                    ).then_inc(S["a1_ready"], 1)

            def make_d1(i, c):
                b = 2 * i + c
                wait(dve, "dw_done", b + 1)
                wait(dve, "gt_done", b)
                wait(dve, "ds_ready", b + 1)
                for h in range(2):
                    cols = slice(2 * P * h, 2 * P * (h + 1))
                    v.tensor_tensor(d1[:, cols], bank[5][:, cols], ds[:, c % 2, cols], ALU.mult
                                    ).then_inc(S["d1_ready"], 1)

            def clip_err(i, c):
                b = 2 * i + c
                for h in range(2):
                    dve.wait_ge(S["err_done"], 2 * b + h + 1)
                    if h == 0:
                        wait(dve, "g1_done", b)
                    v.tensor_scalar(halves(er[:])[h], err_half(h), ERR_CLIP, -ERR_CLIP,
                                    ALU.min, ALU.max).then_inc(S["clip_ready"], 1)

            def rest_xn(i, c):
                b = 2 * i + c
                dve.wait_ge(S["xt_hi_ready"], b + 1)
                v.tensor_tensor(f32r(xt_lo[:]), bank[0][:], xt_hi[:], ALU.subtract).then_inc(S["xt_lo_ready"], 1)

            v.memset(zeros[:], 0.0).then_inc(S["zeros_ready"], 1)
            for k, s in enumerate(from_one):
                v.memset(started[:, k:k + 1], 0.0).then_inc(S[s], 1)
            stats(0, 0)
            stats(0, 1)
            normalise(0, 0)
            dve.wait_ge(S["wts_loaded"], 16)
            v.tensor_scalar(f32r(av_hi[:, P:]), w(WVT), -1.0, None, ALU.mult).then_inc(S["setup_ready"], 1)
            dve.wait_ge(S["setup_ready"], 1)
            v.scalar_tensor_tensor(out=f32r(av_lo[:, P:]), in0=w(WVT), scalar=-1.0, in1=av_hi[:, P:],
                                   op0=ALU.mult, op1=ALU.subtract).then_inc(S["setup_ready"], 1)
            dve.wait_ge(S["setup_mm"], 1)
            v.tensor_copy(f32r(av_hi[:, 0:P]), bank[7][:, 0:P]).then_inc(S["setup_ready"], 1)
            dve.wait_ge(S["setup_ready"], 3)
            v.tensor_tensor(f32r(av_lo[:, 0:P]), bank[7][:, 0:P], av_hi[:, 0:P], ALU.subtract
                            ).then_inc(S["setup_ready"], 1)
            rest_xn(0, 0)
            dve.wait_ge(S["setup_mm"], 2)
            v.tensor_copy(wr_c[:], bank[5][:, 0:E]).then_inc(S["setup_ready"], 1)
            normalise(0, 1)
            make_a1(0, 0)
            clip_err(0, 0)
            rest_xn(0, 1)
            v.memset(empty[:], 0.0).then_inc(S["empty_ready"], 1)
            dve.wait_ge(S["empty_ready"], 1)
            v.memset(empty[:, :, C_ID:C_ID + 1].bitcast(I32), int(NO_TOKEN)).then_inc(S["empty_ready"], 1)
            dve.wait_ge(S["small_loaded"], 32)
            for k in range(3):
                v.tensor_copy(gate_w[:, k * P:(k + 1) * P], gw[:, k:k + 1].to_broadcast([P, P])
                              ).then_inc(S["dve_consts"], 1)
            with dve.Fori(0, NB // 2 - 1) as i:
                for c in (1, 2):
                    stats(i, c + 1)
                    make_a1(i, c)
                    make_d1(i, c - 1)
                    normalise(i, c + 1)
                    clip_err(i, c)
                    rest_xn(i, c + 1)
            dve.wait_ge(S["gates_mm"], 1)
            v.reduce_sum(gl[:], bank[1][:, 0:3 * NB].rearrange("p (g b) -> p g b", g=3), AX
                         ).then_inc(S["gate_step"], 1)
            dve.wait_ge(S["gate_step"], 1)
            v.scalar_tensor_tensor(out=gp[:], in0=gl[:], scalar=1.0 / T, in1=gate_b[:], op0=ALU.mult,
                                   op1=ALU.add).then_inc(S["gate_step"], 1)
            make_a1(0, NB - 1)
            make_d1(0, NB - 2)
            dve.wait_ge(S["gates_ready"], 1)
            v.tensor_scalar(gk[:, 0:1], gs[:, 0:1], -1.0, 1.0, ALU.mult, ALU.add)
            v.tensor_scalar(gk[:, 1:2], gs[:, 1:2], -SCALE, None, ALU.mult)
            v.tensor_scalar(gk[:, 2:3], gs[:, 2:3], 0.0, None, ALU.mult).then_inc(S["upd_step"], 1)
            dve.wait_ge(S["upd_step"], 1)
            v.tensor_scalar(base0[:], w(W0T), gk[:, 0:1], gk[:, 2:3], ALU.mult, ALU.add)
            v.tensor_scalar(base1[:], w(W1N), gk[:, 0:1], gk[:, 2:3], ALU.mult, ALU.add
                            ).then_inc(S["upd_step"], 1)
            dve.wait_ge(S["consts_ready"], 7)
            v.tensor_copy(rank[:], rank[:].bitcast(I32)).then_inc(S["dve_consts"], 1)
            v.memset(hot[:, 0, 0, :], 0.0).then_inc(S["dve_consts"], 1)
            clip_err(0, NB - 1)
            wait(dve, "ds_ready", NB)
            wait(dve, "gt_done", NB - 1)
            for h in range(2):
                cols = slice(2 * P * h, 2 * P * (h + 1))
                wait(dve, "dw_done", NB + h)
                v.tensor_tensor(d1[:, cols], back_of_half(h), ds[:, (NB - 1) % 2, cols], ALU.mult
                                ).then_inc(S["d1_ready"], 1)
            LIMIT = GRAD_CLIP / SCALE
            wait(dve, "gt_done", NB)
            v.tensor_copy(gt[:], bank[6][:, P:2 * P]).then_inc(S["gt_ready"], 1)
            v.tensor_scalar(c1[:], bank[6][:, 0:P], LIMIT, -LIMIT, ALU.min, ALU.max).then_inc(S["upd_step"], 1)
            dve.wait_ge(S["upd_step"], 3)
            v.scalar_tensor_tensor(out=w1n[:], in0=c1[:], scalar=gk[:, 1:2], in1=base1[:], op0=ALU.mult,
                                   op1=ALU.add).then_inc(S["w1_ready"], 1)
            dve.wait_ge(S["g0_mm"], 1)
            v.tensor_scalar(c0[:], bank[7][:, 0:P], LIMIT, -LIMIT, ALU.min, ALU.max).then_inc(S["upd_step"], 1)
            dve.wait_ge(S["upd_step"], 4)
            v.scalar_tensor_tensor(out=w0n[:], in0=c0[:], scalar=gk[:, 1:2], in1=base0[:], op0=ALU.mult,
                                   op1=ALU.add).then_inc(S["w0_ready"], 1)
            dve.wait_ge(S["mz_mm"], 2)
            v.tensor_copy(mz[:], bank[7][:, 0:P]).then_inc(S["mz_ready"], 1)

            def router(i, c):
                b = 2 * i + c
                lg = bank[3][:, 0:GROUP * E].rearrange("p (g e) -> p g e", e=E)
                ps = bank[4][:, 0:GROUP * E].rearrange("p (g e) -> p g e", e=E)
                d = rows[:, bass.ds(GROUP * b, GROUP), C_D:C_D + E]

                def wide(t):
                    return t[:].rearrange("p (g o) -> p g o", o=1).to_broadcast([P, GROUP, E])

                def s0():
                    dve.wait_ge(S["lg_done"], b + 1)
                    v.reduce_max(mx[:], lg, AX).then_inc(S["mx_ready"], 1)

                def s1():
                    dve.wait_ge(S["mx_ready"], b + 1)
                    v.tensor_tensor(d, lg, wide(mx), ALU.subtract).then_inc(S["d_ready"], 1)

                def s2():
                    dve.wait_ge(S["d_ready"], b + 1)
                    v.scalar_tensor_tensor(
                        out=cand[:], in0=d, scalar=0.0,
                        in1=rank[:].rearrange("p (o e) -> p o e", o=1).to_broadcast([P, GROUP, E]),
                        op0=ALU.is_ge, op1=ALU.mult).then_inc(S["cand_ready"], 1)

                def s3():
                    dve.wait_ge(S["cand_ready"], b + 1)
                    v.reduce_max(best[:], cand[:], AX).then_inc(S["best_ready"], 1)

                def s4():
                    dve.wait_ge(S["best_ready"], b + 1)
                    v.tensor_tensor(hot[:, c % 2, 1:, :], cand[:], wide(best), ALU.is_equal
                                    ).then_inc(S["hot_ready"], 1)

                def s5():
                    dve.wait_ge(S["hot_ready"], b + 1)
                    with nc.allow_low_precision("counts up to 32 are exact in bfloat16"):
                        v.reduce_sum(hot[:, 1 - c % 2, 0, :], hot[:, c % 2].rearrange("p g e -> p e g"), AX
                                     ).then_inc(S["count_ready"], 1)

                def s6():
                    dve.wait_ge(S["pos_mm"], b + 1)
                    v.tensor_tensor(own[:], ps, hot[:, c % 2, 1:, :], ALU.mult).then_inc(S["own_ready"], 1)

                def s7():
                    dve.wait_ge(S["own_ready"], b + 1)
                    v.reduce_sum(pos[:], own[:], AX).then_inc(S["pos_ready"], 1)

                def s8():
                    dve.wait_ge(S["pos_ready"], b + 1)
                    v.scalar_tensor_tensor(out=slot[:], in0=best[:], scalar=-float(CAP), in1=pos[:],
                                           op0=ALU.mult, op1=ALU.add).then_inc(S["slot_ready"], 1)
                    v.tensor_scalar(over[:], pos[:], float(CAP), NO_SLOT, ALU.is_ge, ALU.mult
                                    ).then_inc(S["over_ready"], 1)

                def s9():
                    dve.wait_ge(S["over_ready"], b + 1)
                    v.scalar_tensor_tensor(out=idx[:, bass.ds(GROUP * b, GROUP)], in0=slot[:],
                                           scalar=float(E * CAP), in1=over[:], op0=ALU.add, op1=ALU.add
                                           ).then_inc(S["idx_ready"], 1)

                return [s0, s1, s2, s3, s4, s5, s6, s7, s8, s9]

            def stats2(i, c):
                b = 2 * i + c

                def one(k):
                    def step():
                        if k == 0:
                            wait(dve, "mv2_ready", 2 * b)
                            dve.wait_ge(S["x1_ready"], b + 1)
                            carry()
                        ins = v.bn_stats(stat2[:, k, :], rows[:, bass.ds(GROUP * b + k, 1), 0:D
                                                              ].rearrange("p a d -> p (a d)"))
                        if k == GROUP - 1:
                            ins.then_inc(S["stat2_done"], 1)
                    return step

                def aggr(k):
                    def step():
                        if k == 0:
                            dve.wait_ge(S["stat2_done"], b + 1)
                            carry()
                        ins = v.bn_aggr(mv2[:, k, :], stat2[:, k, :])
                        if k == GROUP - 1:
                            ins.then_inc(S["mv2_ready"], 1)
                    return step

                def put():
                    dve.wait_ge(S["mv2_ready"], 2 * b + 1)
                    v.tensor_copy(rows[:, bass.ds(GROUP * b, GROUP), C_MEAN:C_VAR + 1], mv2[:]
                                  ).then_inc(S["mv2_ready"], 1)

                return [one(k) for k in range(GROUP)], [aggr(k) for k in range(GROUP)] + [put]

            def second(i, c, first=False, last=False):
                r = router(i, c)
                s, g = stats2(i, c + 1)
                if last:
                    order = r
                elif first:
                    order = r + s + g
                else:
                    order = r[:5] + [s[0], r[5], s[1], r[6], s[2], r[7], s[3], r[8], g[0], r[9]] + g[1:]
                for step in order:
                    step()

            dve.wait_ge(S["dve_consts"], 5)
            s, g = stats2(0, 0)
            for step in s + g:
                step()
            second(0, 0, first=True)
            with dve.Fori(0, NB // 2 - 1) as i:
                second(i, 1)
                second(i, 2)
            second(0, NB - 1, last=True)

            def weights_lo(e):
                dve.wait_ge(S["hi_ready"], e + 1)
                v.tensor_tensor(f32r(w1_lo[:, e, :]), centre_bank(e), w1_hi[:, e, :], ALU.subtract
                                ).then_inc(S["lo_ready"], 1)

            for e in range(E):
                weights_lo(e)

            def base_scales(h):
                k = slice(TILES // 2 * h, TILES // 2 * (h + 1))
                dve.wait_ge(S["rs2_ready"], h + 1)
                v.tensor_scalar(rs2p[:, k], rs2[:, k], 1.0, None, ALU.add).then_inc(S["nm_ready"], 1)
                v.scalar_tensor_tensor(out=nmr2[:, k], in0=rs2[:, k], scalar=-1.0, in1=rows[:, k, C_MEAN],
                                       op0=ALU.mult, op1=ALU.mult).then_inc(S["nm_ready"], 2)
                dve.wait_ge(S["nm_ready"], 3 * (h + 1))

            def base_rows(q):
                for k in range(BT * q, BT * (q + 1)):
                    ins = v.tensor_scalar(tile(xr, k), rows[:, k, 0:D], rs2p[:, k:k + 1], nmr2[:, k:k + 1],
                                          ALU.mult, ALU.add)
                ins.then_inc(S["base_ready_v"], 1)

            def of(e, part):
                return dr[:, bass.ds(e, 1), :, part].rearrange("p e s c -> p (e s) c")

            def rest_t(i, c):
                e = 2 * i + c
                for n in range(2):
                    dve.wait_ge(S["tt_hi_ready"], 2 * e + n + 1)
                    v.tensor_tensor(f32r(tt_lo[:, part_cols(n)]), turned_part(n), tt_hi[:, part_cols(n)],
                                    ALU.subtract).then_inc(S["tt_lo_ready"], 1)

            def scaled(i, c):
                e = 2 * i + c
                wait(dve, "th_ready", e)
                dve.wait_ge(S["rs3_ready"], e + 1)
                v.tensor_tensor(dd[:], of(e, slice(C_D, C_D + E)),
                                rs3[:, c % 2].rearrange("p (s o) -> p s o", o=1).to_broadcast([P, ST, E]),
                                ALU.mult).then_inc(S["dd_ready"], 1)

            def pmax(i, c):
                e = 2 * i + c
                dve.wait_ge(S["th_ready"], e + 1)
                v.tensor_scalar(den[:], th[:], -1.0, 1.0, ALU.mult, ALU.add).then_inc(S["den_ready"], 1)
                dve.wait_ge(S["den_ready"], e + 1)
                v.reciprocal(rat[:], den[:]).then_inc(S["rat_ready"], 1)
                dve.wait_ge(S["rat_ready"], e + 1)
                v.scalar_tensor_tensor(out=den[:], in0=th[:], scalar=1.0, in1=rat[:], op0=ALU.add,
                                       op1=ALU.mult).then_inc(S["esum_ready"], 1)
                dve.wait_ge(S["esum_ready"], 2 * e + 1)
                v.reduce_sum(esum[:], den[:], AX).then_inc(S["esum_ready"], 1)
                dve.wait_ge(S["esum_ready"], 2 * e + 2)
                v.reciprocal(pm[:], esum[:]).then_inc(S["pm_ready"], 1)
                wait(dve, "fin_ready", ST * e)
                dve.wait_ge(S["pm_ready"], e + 1)
                v.tensor_tensor(yscale[:], pm[:], rs3[:, c % 2], ALU.mult).then_inc(S["yscale_ready"], 1)

            def finish(i, c, first, ending):
                e = 2 * i + c
                if not first:
                    dve.wait_ge(sent[c % 2], 16 * ST * (i + c // 2))
                v.tensor_copy(ids[:, c % 2].rearrange("p (s o) -> p s o", o=1),
                              of(e, slice(C_ID, C_ID + 1)).bitcast(I32))
                dve.wait_ge(S["yscale_ready"], e + 1)
                row = of(e, slice(0, ROW))
                for s in range(ST):
                    y, start, last = y_tile(s, ending)
                    if s == start:
                        dve.wait_ge(S["y_mm"], ST * e + last + 1)
                    v.scalar_tensor_tensor(out=orow[:, c % 2, s, :], in0=y, scalar=yscale[:, s:s + 1],
                                           in1=row[:, s, 0:D], op0=ALU.mult, op1=ALU.add
                                           ).then_inc(S["fin_ready"], 1)

            def expert(i, c, first=False, last=False):
                pmax(i, c)
                if not last:
                    rest_t(i, c + 1)
                    scaled(i, c + 1)
                finish(i, c, first, last)

            base_scales(0)
            base_rows(0)
            rest_t(0, 0)
            base_rows(1)
            base_scales(1)
            base_rows(2)
            scaled(0, 0)
            expert(0, 0, first=True)
            expert(0, 1, first=True)
            with dve.Fori(0, E // 2 - 2) as i:
                expert(i, 2)
                expert(i, 3)
            expert(0, E - 2)
            expert(0, E - 1, last=True)

        @block.tensor
        def _(pe):
            t = nc.tensor

            def turn(dst, src, n=GROUP):
                for k in range(n):
                    ins = t.transpose(tile(dst, k), tile(src, k), ident[:])
                return ins

            def turn_xn(i, c):
                b = 2 * i + c
                wait(pe, "xnt_ready", b)
                pe.wait_ge(S["xn_ready"], b + 1)
                turn(bank[0], xn[:, c % 2]).then_inc(S["xt_done"], 1)

            def pre(i, c):
                b = 2 * i + c
                wait(pe, "clip_ready", 2 * b)
                pe.wait_ge(S["xt_hi_ready"], b + 1)
                for k in range(GROUP):
                    t.matmul(pair(k), f32r(tile(xt_hi, k)), f32r(av_hi[:]), start=(k % 2 == 0), stop=False,
                             skip_group_check=True)
                    t.matmul(pair(k), f32r(tile(xt_hi, k)), f32r(av_lo[:]), start=False, stop=False,
                             skip_group_check=True)
                pe.wait_ge(S["xt_lo_ready"], b + 1)
                for k in range(GROUP):
                    ins = t.matmul(pair(k), f32r(tile(xt_lo, k)), f32r(av_hi[:]), start=False, stop=False,
                                   skip_group_check=True)
                    if k % 2:
                        ins.then_inc(S["pre_done"], 1)

            def turn_a1(i, c):
                b = 2 * i + c
                wait(pe, "a1t_ready", b)
                for k in range(GROUP):
                    if k % 2 == 0:
                        pe.wait_ge(S["a1_ready"], 2 * b + k // 2 + 1)
                    ins = t.transpose(tile(bank[2], k), tile(a1[:, c % 2], k), ident[:])
                ins.then_inc(S["at_done"], 1)

            def err(i, c):
                b = 2 * i + c
                pe.wait_ge(S["a1t_ready"], b + 1)
                for k in range(GROUP):
                    ins = t.matmul(pair(k)[:, P:2 * P], tile(a1t, k), w(W1T), start=False, stop=True,
                                   skip_group_check=True)
                    if k % 2:
                        ins.then_inc(S["err_done"], 1)

            def turn_err(i, c):
                b = 2 * i + c
                wait(pe, "ert_ready", b)
                pe.wait_ge(S["clip_ready"], 2 * b + 1)
                for k in range(GROUP):
                    if k == 2:
                        pe.wait_ge(S["clip_ready"], 2 * b + 2)
                    ins = t.transpose(tile(bank[4], k), tile(er, k), ident[:])
                ins.then_inc(S["et_done"], 1)

            def back(i, c):
                b = 2 * i + c
                wait(pe, "d1_ready", 2 * b)
                wait(pe, "ert_ready", b + 1)
                for k in range(GROUP):
                    ins = t.matmul(tile(bank[5], k), tile(ert, k), w(W1N), start=True, stop=True)
                ins.then_inc(S["dw_done"], 1)

            def grad1_tiles(i, c, tiles):
                for k in tiles:
                    ins = t.matmul(bank[6][:, 0:P], tile(er, k), tile(a1[:, c % 2], k), start=False, stop=False,
                                   skip_group_check=True)
                return ins

            def grad0_tiles(i, c, tiles):
                for k in tiles:
                    ins = t.matmul(bank[6][:, P:2 * P], tile(xn[:, c % 2], k), tile(d1, k), start=False,
                                   stop=False, skip_group_check=True)
                return ins

            def grad0(i, c):
                b = 2 * i + c
                wait(pe, "d1_ready", 2 * b + 1)
                grad0_tiles(i, c, (0, 1))
                wait(pe, "d1_ready", 2 * b + 2)
                grad0_tiles(i, c, (2, 3)).then_inc(S["gt_done"], 1)

            def turn_err_half(h):
                pe.wait_ge(S["clip_ready"], 2 * (NB - 1) + h + 1)
                for k in (0, 1):
                    ins = t.transpose(tile(turned_half(h), k), tile(er, 2 * h + k), ident[:])
                ins.then_inc(S["et_done"], 1)

            def back_half(h):
                wait(pe, "ert_ready", NB + h)
                for k in (0, 1):
                    ins = t.matmul(tile(back_of_half(h), k), tile(ert, 2 * h + k), w(W1N), start=True, stop=True)
                ins.then_inc(S["dw_done"], 1)

            def grad0_half(h):
                wait(pe, "d1_ready", 2 * (NB - 1) + h + 1)
                return grad0_tiles(0, NB - 1, (2 * h, 2 * h + 1))

            def keep_clock(n, b):
                for _ in range(n):
                    t.matmul(bank[b][:, 0:2 * P], zeros[:, 0:P], zeros[:], start=True, stop=True)

            pe.wait_ge(S["zeros_ready"], 1)
            t.matmul(bank[6][:, 0:2 * P], zeros[:, 0:P], zeros[:], start=True, stop=True)
            keep_clock(5, 7)
            pe.wait_ge(S["ident_ready"], 2)
            turn_xn(0, 0)
            pe.wait_ge(S["wts_loaded"], 16)
            t.matmul(bank[7][:, 0:P], w(WK), w(W0T), start=True, stop=True).then_inc(S["setup_mm"], 1)
            pe.wait_ge(S["consts_ready"], 3)
            pe.wait_ge(S["small_loaded"], 32)
            t.matmul(bank[5][:, 0:E], centre[:], gw[:, 3:3 + E], start=True, stop=True
                     ).then_inc(S["setup_mm"], 1)
            pe.wait_ge(S["setup_ready"], 4)
            pre(0, 0)
            turn_xn(0, 1)
            turn_a1(0, 0)
            err(0, 0)
            with pe.Fori(0, NB // 2 - 1) as i:
                for c in (1, 2):
                    turn_err(i, c - 1)
                    grad1_tiles(i, c - 1, (0, 1))
                    pre(i, c)
                    back(i, c - 1)
                    grad1_tiles(i, c - 1, (2, 3)).then_inc(S["g1_done"], 1)
                    turn_a1(i, c)
                    grad0(i, c - 1)
                    err(i, c)
                    turn_xn(i, c + 1)
            turn_err(0, NB - 2)
            grad1_tiles(0, NB - 2, (0, 1))
            pre(0, NB - 1)
            pe.wait_ge(S["dve_consts"], 3)
            pe.wait_ge(S["xnt_ready"], NB)
            for k in range(3):
                ins = t.matmul(bank[1][:, k * NB:(k + 1) * NB], tile(gate_w, k), xsum[:], start=True, stop=True)
            ins.then_inc(S["gates_mm"], 1)
            back(0, NB - 2)
            grad1_tiles(0, NB - 2, (2, 3)).then_inc(S["g1_done"], 1)
            turn_a1(0, NB - 1)
            grad0(0, NB - 2)
            pe.wait_ge(S["gate_step"], 1)
            err(0, NB - 1)
            turn_err_half(0)
            grad1_tiles(0, NB - 1, (0, 1))
            turn_err_half(1)
            back_half(0)
            grad1_tiles(0, NB - 1, (2, 3)).then_inc(S["g1_done"], 1)
            back_half(1)
            grad0_half(0)
            grad0_half(1).then_inc(S["gt_done"], 1)
            keep_clock(1, 4)
            pe.wait_ge(S["gt_ready"], 1)
            t.matmul(bank[7][:, 0:P], w(WKT), gt[:], start=True, stop=True).then_inc(S["g0_mm"], 1)
            pe.wait_ge(S["w1_ready"], 1)
            t.matmul(bank[5][:, 0:P], w1n[:], w(WOT), start=True, stop=True).then_inc(S["mz_mm"], 1)
            keep_clock(1, 4)
            pe.wait_ge(S["w0_ready"], 1)
            t.matmul(bank[7][:, 0:P], w(WQ), w0n[:], start=True, stop=True).then_inc(S["mz_mm"], 1)
            keep_clock(1, 4)

            def hidden(i, c):
                b = 2 * i + c
                wait(pe, "silu_ready", b)
                t.matmul(bank[0][:], mz[:], xnt_all[:, bass.ds(COLS * b, COLS)], start=True, stop=True
                         ).then_inc(S["z_done"], 1)

            def output(i, c):
                b = 2 * i + c
                pe.wait_ge(S["silu_ready"], b + 1)
                for k in range(GROUP):
                    ins = t.matmul(tile(bank[1], k), tile(st, k), n2[:], start=False, stop=True,
                                   skip_group_check=True)
                ins.then_inc(S["o_done"], 1)

            def residual(i, c):
                b = 2 * i + c
                wait(pe, "x1_ready", b)
                t.matmul(bank[1][:], ident[:], xr[:, bass.ds(COLS * b, COLS)], start=True, stop=False,
                         skip_group_check=True)

            def turn_x1(i, c):
                b = 2 * i + c
                wait(pe, "x1t_ready", b)
                pe.wait_ge(S["x1_ready"], b + 1)
                for k in range(GROUP):
                    ins = t.transpose(tile(bank[2], k), x1_tile(i, c, k), ident[:])
                ins.then_inc(S["x1t_done"], 1)

            def x1_tile(i, c, k):
                return rows[:, GROUP * (2 * i + c) + k, 0:D]

            def logits(i, c):
                b = 2 * i + c
                wait(pe, "d_ready", b)
                pe.wait_ge(S["x1t_ready"], b + 1)
                for k in range(GROUP):
                    ins = t.matmul(bank[3][:, k * E:(k + 1) * E], tile(x1t, k), wr_c[:], start=True, stop=True)
                ins.then_inc(S["lg_done"], 1)

            def positions(i, c):
                b = 2 * i + c
                wait(pe, "count_ready", b)
                wait(pe, "own_ready", b)
                pe.wait_ge(S["hot_ready"], b + 1)
                ps = bank[4][:, 0:GROUP * E]
                h = hot[:, c % 2]
                t.matmul(ps, upper[:], h[:, 1:, :].rearrange("p g e -> p (g e)"), start=True, stop=False)
                for k in range(GROUP):
                    n = GROUP - k
                    ins = t.matmul(ps[:, k * E:].rearrange("p (g e) -> p g e", e=E), ones[:],
                                   h[:, k:k + 1, :].to_broadcast([P, n, E]), start=False,
                                   stop=(k == GROUP - 1))
                ins.then_inc(S["pos_mm"], 1)

            pe.wait_ge(S["mz_ready"], 1)
            hidden(0, 0)
            residual(0, 0)
            pe.wait_ge(S["n2_ready"], 1)
            output(0, 0)
            hidden(0, 1)
            pe.wait_ge(S["consts_ready"], 6)
            turn_x1(0, 0)
            residual(0, 1)
            logits(0, 0)
            output(0, 1)
            for b in range(NB - 2):
                hidden(0, b + 2)
                positions(0, b)
                turn_x1(0, b + 1)
                residual(0, b + 2)
                logits(0, b + 1)
                output(0, b + 2)

            def centre_w(e):
                wait(pe, "lo_ready", e - 3)
                t.matmul(centre_bank(e), centre[:], w1_in[:, F * e:F * (e + 1)], start=True, stop=True
                         ).then_inc(S["centred"], 1)

            positions(0, NB - 2)
            turn_x1(0, NB - 1)
            pe.wait_ge(S["w_up_loaded"], 16)
            pe.wait_ge(S["silu_ready"], NB)
            centre_w(0)
            logits(0, NB - 1)
            centre_w(1)
            positions(0, NB - 1)
            for e in range(2, E):
                centre_w(e)

            def turn_t(e):
                wait(pe, "tt_lo_ready", 2 * e)
                for n in range(2):
                    if e == n == 0:
                        pe.wait_ge(S["first_rows"], 16)
                    else:
                        pe.wait_ge(dr_loaded[e % 2], 16 * (e // 2 + 1))
                    for k, s in enumerate(parts[n]):
                        ins = t.transpose(tile(turned_part(n), k), dr[:, e, s, 0:D], ident[:])
                    ins.then_inc(S["tt_mm"], 1)

            def layer1(e, half, spread=False):
                cols = slice(half * HALF, (half + 1) * HALF)

                def place(f):
                    return bank[f][:, 0:HALF], f32r(tile(w1_hi[:, e], f)), f32r(tile(w1_lo[:, e], f))

                def with_hi(f):
                    o, hi, lo = place(f)
                    t.matmul(o, hi, f32r(tt_hi[:, cols]), start=True, stop=False)
                    t.matmul(o, lo, f32r(tt_hi[:, cols]), start=False, stop=False)

                def with_lo(f):
                    o, hi, lo = place(f)
                    t.matmul(o, hi, f32r(tt_lo[:, cols]), start=False, stop=True).then_inc(S["h_mm"], 1)

                pe.wait_ge(S["tt_hi_ready"], 2 * e + half + 1)
                if spread:
                    for f in range(FC):
                        with_hi(f)
                pe.wait_ge(S["tt_lo_ready"], 2 * e + half + 1)
                for f in range(FC):
                    if half == 0 and f == 3:
                        wait(pe, "fin_ready", ST * e)
                    if half == 1:
                        pe.wait_ge(S["h_ready"], 2 * FC * e + f + 1)
                    if not spread:
                        with_hi(f)
                    with_lo(f)

            def layer2(e, ending):
                for s in range(ST):
                    if s == 0:
                        pe.wait_ge(S["h_ready"], 2 * FC * e + FC)
                    if (s + 1) * P > HALF >= s * P:
                        pe.wait_ge(S["h_ready"], 2 * FC * (e + 1))
                    y, start, last = y_tile(s, ending)
                    if s == start:
                        wait(pe, "fin_ready", ST * e + 1 if ending and s == 4 else ST * (e - 1) + last + 1)
                    for f in range(FC):
                        ins = t.matmul(y, ht[:, f, s * P:(s + 1) * P], w2[:, e, f, :],
                                       start=(f == 0), stop=(f == FC - 1))
                    if s == last:
                        ins.then_inc(S["y_mm"], last - start + 1)

            pe.wait_ge(S["lo_ready"], E)
            keep_clock(9, 4)
            turn_t(0)
            keep_clock(1, 4)
            pe.wait_ge(S["w_down_loaded"], 16)
            for e in range(E):
                last = e == E - 1
                layer1(e, 0, spread=(e == 0))
                layer1(e, 1)
                if not last:
                    turn_t(e + 1)
                layer2(e, ending=last)


def kernel(**inputs):
    import concourse.bacc as bacc
    from concourse.bass_utils import run_bass_kernel_spmd

    a = {k.removeprefix("L0_"): np.asarray(v) for k, v in inputs.items()}
    x = a["attn_x"]
    Wk, Wv, Wq, Wout, W0, W1 = (a["attn_" + n] for n in ("Wk", "Wv", "Wq", "Wout", "W0", "W1"))
    arrays = {
        "x": np.ascontiguousarray(x.reshape(-1, x.shape[-1])),
        "wpack": np.ascontiguousarray(np.concatenate([Wk, Wk.T, Wv.T, Wq, W0.T, W1, W1.T, Wout.T], axis=1)),
        "wsmall": np.ascontiguousarray(np.concatenate(
            [a["attn_Wg_decay"].T, a["attn_Wg_lr"].T, a["attn_Wg_mom"].T, a["ffn_Wr"]], axis=1)),
        "biases": np.concatenate([a["attn_bg_decay"], a["attn_bg_lr"], a["attn_bg_mom"]])[None, :],
        "w_up": np.ascontiguousarray(a["ffn_W1"]),
        "w_down": np.ascontiguousarray(a["ffn_W2"]),
    }
    nc = bacc.Bacc("TRN2", target_bir_lowering=False, num_devices=1)
    args = [nc.dram_tensor(f"in_{n}", v.shape, mybir.dt.from_np(v.dtype), kind="ExternalInput").ap()
            for n, v in arrays.items()]
    y = nc.dram_tensor("out_y", arrays["x"].shape, F32, kind="ExternalOutput").ap()
    build(nc, *args, y)
    r = run_bass_kernel_spmd(nc, [{f"in_{n}": v for n, v in arrays.items()}], core_ids=[0])
    return r.results[0]["out_y"].reshape(x.shape)
```
